# Optimizing a Trainium2 kernel written in Bass

```python
import numpy as np
import jax
import jax.numpy as jnp

def _softmax(x, axis=-1):
    return jax.nn.softmax(x, axis=axis)
def _gelu(x):
    return jax.nn.gelu(x, approximate=True)
def _silu(x):
    return jax.nn.silu(x)
def _sigmoid(x):
    return jax.nn.sigmoid(x)
def _layernorm(x, axis=-1, eps=1e-5):
    m = jnp.mean(x, axis=axis, keepdims=True)
    v = jnp.var(x, axis=axis, keepdims=True)
    return (x - m) / jnp.sqrt(v + eps)
def _scatter_add(tgt, idx, src, axis=0):
    return tgt.at[idx].add(src)
def _segment_sum(src, seg, n):
    return jax.ops.segment_sum(src, seg, n)

kernel_name = 'mk_conv_seq_d2_conv_nchw512_d00502'

def setup_inputs(seed: int = 0):
    np.random.seed(seed)
    _w = jnp.asarray
    def _rec_inputs():
        import jax
        import jax.numpy as jnp
        _gk = jax.random.key(seed)
        x = -9.26e-05 + 0.9999 * jax.random.normal(jax.random.fold_in(_gk, 1), (8, 512, 96, 96), jnp.float32)
        return x
    x = _rec_inputs()
    def _L0_conv_setup():
        import jax, jax.numpy as jnp
        import numpy as np
        N, C, H, W = (8, 512, 96, 96)
        CQK = C // 8
        NEG = -1e+30
        key = jax.random.key(seed)
        ks = jax.random.split(key, 8)
        s = 0.02
        return {'x': jax.random.normal(ks[0], (N, C, H, W), dtype=jnp.float32), 'wq': jax.random.normal(ks[1], (CQK, C), dtype=jnp.float32) * s, 'bq': jax.random.normal(ks[2], (CQK,), dtype=jnp.float32) * s, 'wk': jax.random.normal(ks[3], (CQK, C), dtype=jnp.float32) * s, 'bk': jax.random.normal(ks[4], (CQK,), dtype=jnp.float32) * s, 'wv': jax.random.normal(ks[5], (C, C), dtype=jnp.float32) * s, 'bv': jax.random.normal(ks[6], (C,), dtype=jnp.float32) * s, 'gamma': jnp.float32(0.5)}
    _L0_conv_all = _L0_conv_setup()
    _L0_conv_in = {k: v for k, v in _L0_conv_all.items() if k in ('wq', 'bq', 'wk', 'bk', 'wv', 'bv', 'gamma', )}
    del _L0_conv_all

    def _L1_conv_setup():
        import jax, jax.numpy as jnp
        import numpy as np
        import jax.scipy.linalg as jsl
        EPS = 0.001
        GROUP_SIZE = 16
        key = jax.random.key(seed)
        x = jax.random.normal(key, (32, 512, 56, 56), dtype=jnp.float32)
        return {'x': x}
    _L1_conv_all = _L1_conv_setup()
    _L1_conv_in = {k: v for k, v in _L1_conv_all.items() if k in ()}
    del _L1_conv_all

    return {
        "x": x,
        "L0_conv_wq": _L0_conv_in["wq"],
        "L0_conv_bq": _L0_conv_in["bq"],
        "L0_conv_wk": _L0_conv_in["wk"],
        "L0_conv_bk": _L0_conv_in["bk"],
        "L0_conv_wv": _L0_conv_in["wv"],
        "L0_conv_bv": _L0_conv_in["bv"],
        "L0_conv_gamma": _L0_conv_in["gamma"],
    }

def reference(x, L0_conv_wq, L0_conv_bq, L0_conv_wk, L0_conv_bk, L0_conv_wv, L0_conv_bv, L0_conv_gamma):
    import jax
    import jax.numpy as jnp
    def _L0_conv_ref(x, wq, bq, wk, bk, wv, bv, gamma):
        import jax, jax.numpy as jnp
        import numpy as np
        N, C, H, W = (8, 512, 96, 96)
        CQK = C // 8
        NEG = -1e+30
        q = jnp.einsum('nchw,oc->nohw', x, wq) + bq[None, :, None, None]
        k = jnp.einsum('nchw,oc->nohw', x, wk) + bk[None, :, None, None]
        v = jnp.einsum('nchw,oc->nohw', x, wv) + bv[None, :, None, None]
        h, w = (q.shape[2], q.shape[3])
        e_row = jnp.einsum('ncyx,ncyi->niyx', q, k)
        e_col = jnp.einsum('ncyx,ncix->niyx', q, k)
        diag = jnp.eye(h, dtype=bool)[None, :, :, None]
        e_col = jnp.where(diag, NEG, e_col)
        energy = jnp.concatenate([e_row, e_col], axis=1)
        attn = jax.nn.softmax(energy, axis=1)
        a_row, a_col = (attn[:, :w], attn[:, w:])
        out = jnp.einsum('niyx,ncyi->ncyx', a_row, v) + jnp.einsum('niyx,ncix->ncyx', a_col, v)
        return gamma * out + x

    def _L1_conv_ref(x):
        import jax, jax.numpy as jnp
        import numpy as np
        import jax.scipy.linalg as jsl
        EPS = 0.001
        GROUP_SIZE = 16
        B, C, H, W = x.shape
        gs = GROUP_SIZE
        G = C // gs
        m = jnp.mean(x, axis=(0, 2, 3), keepdims=True)
        xn = x - m
        T = jnp.transpose(xn, (1, 0, 2, 3)).reshape(G, gs, -1)
        N = T.shape[-1]
        f_cov = jnp.einsum('gin,gjn->gij', T, T) / N
        eye = jnp.eye(gs, dtype=x.dtype)
        f_cov_shrinked = (1.0 - EPS) * f_cov + EPS * eye
        L = jnp.linalg.cholesky(f_cov_shrinked)
        Linv = jsl.solve_triangular(L, jnp.broadcast_to(eye, (G, gs, gs)), lower=True)
        dec = jnp.einsum('gij,gjn->gin', Linv, T)
        out = jnp.transpose(dec.reshape(C, B, H, W), (1, 0, 2, 3))
        return out

    def _gn(v, G=32, eps=1e-5):
        B_, C_, H_, W_ = v.shape
        g = v.reshape(B_, G, C_ // G, H_, W_)
        m = jnp.mean(g, axis=(2, 3, 4), keepdims=True)
        s = jnp.var(g, axis=(2, 3, 4), keepdims=True)
        return ((g - m) / jnp.sqrt(s + eps)).reshape(v.shape)

    def _ln_c(v, eps=1e-6):
        m = jnp.mean(v, axis=1, keepdims=True)
        s = jnp.var(v, axis=1, keepdims=True)
        return (v - m) / jnp.sqrt(s + eps)

    def _ln_t(v, eps=1e-5):
        m = jnp.mean(v, axis=-1, keepdims=True)
        s = jnp.var(v, axis=-1, keepdims=True)
        return (v - m) / jnp.sqrt(s + eps)

    def _to_tokens(v):
        B_, C_, H_, W_ = v.shape
        return v.reshape(B_, C_, H_ * W_).transpose(0, 2, 1)
    def _from_tokens(t, like):
        B_, C_, H_, W_ = like.shape
        return t.transpose(0, 2, 1).reshape(B_, C_, H_, W_)

    x = _L0_conv_ref(x, L0_conv_wq, L0_conv_bq, L0_conv_wk, L0_conv_bk, L0_conv_wv, L0_conv_bv, L0_conv_gamma)
    x = _L1_conv_ref(x)
    return x


_drawn_inputs = setup_inputs


def setup_inputs(seed=0):
    import zlib

    import numpy as np

    out = dict(_drawn_inputs(seed))
    spreads = {}
    factors = {'L0_conv_bq': 8.0, 'L0_conv_bk': 8.0, 'L0_conv_bv': 8.0}
    for name, (base, spread) in spreads.items():
        noise = np.random.default_rng([zlib.crc32(name.encode()), seed]).standard_normal(out[name].shape)
        drawn = base * np.exp(spread * noise) if base else spread * noise
        out[name] = jnp.asarray(drawn.astype(out[name].dtype))
    for name, factor in factors.items():
        out[name] = (out[name] * factor).astype(out[name].dtype)
    return out
```

```python
from contextlib import ExitStack

import numpy as np

import concourse.bass as bass
from concourse import mybir


def criss_cross_whitening_kernel(nc, x, wq_t, bq, wk_t, bk, wv_t, bv, gamma, out):
    F32 = mybir.dt.float32
    ALU = mybir.AluOpType
    ACT = mybir.ActivationFunctionType
    AX = mybir.AxisListType
    ds = bass.ds

    N, C, H, W = x.shape
    P = 128
    HW = H * W
    D = wq_t.shape[1]
    KC = C // P
    TP = 512
    NT = HW // TP
    SUB = TP // P
    R = 8
    NG = H // R
    RT = 4
    NTR = H // RT
    GS, EPS = 16, 0.001
    GROUPS = C // GS
    BPC = P // GS
    GC = P + 2
    assert H == W and NT % 2 == 0 and NG % 2 == 0 and H % R == 0

    SMALL = 7
    PAIR_READY = NT + 2 * NG + KC * 2 * NG
    PAIR_USES = 2 * NT + 2 * NG + KC * 2 * NG
    BANK_USES = NT + 2 * NTR + KC * NT

    x_px = x.rearrange("n (k p) h w -> n p k (h w)", p=P)
    out_px = out.rearrange("n (k p) h w -> n k p (h w)", p=P)
    v_dram = nc.dram_tensor("v_dram", [N, KC, HW, P], F32)
    y_dram = nc.dram_tensor("y_dram", [N, KC, P, HW], F32)
    v_rows = v_dram[:, :, :, :].rearrange("n k (y x) c -> n k x y c", x=W)
    v_cols = v_dram[:, :, :, :].rearrange("n k (y x) c -> n k y x c", x=W)
    v_tile = v_dram[:, :, :, :].rearrange("n k (q s) c -> n q k (s c)", s=SUB)
    gram_dram = nc.dram_tensor("gram_dram", [C, GC], F32)
    wmat_dram = nc.dram_tensor("wmat_dram", [GROUPS, GS, GS], F32)
    wbias_dram = nc.dram_tensor("wbias_dram", [GROUPS, GS], F32)

    ctx = ExitStack()
    with ctx:
        def sb(name, shape):
            return ctx.enter_context(nc.sbuf_tensor(name, shape, F32))

        def sem(name):
            return ctx.enter_context(nc.semaphore(name))

        qk = sb("qk", [P, 2, HW])
        att = sb("att", [P, 2, HW])
        wqk = sb("wqk", [P, KC, 2 * D])
        wv = sb("wv", [P, KC, C])
        xt = sb("xt", [P, 2, KC, TP])
        ring = sb("ring", [P, 4 * R * P])
        bv_rep = sb("bv_rep", [P, C])
        stage = sb("stage", [P, 2 * R * H + 2 * RT * H])
        ident = sb("ident", [P, P])
        off_diag = sb("off_diag", [H, H])
        stat = sb("stat", [P, 10, H])
        gram_sb = sb("gram_sb", [P, KC, GC])
        cst = sb("cst", [P, 8])

        vout = ring[:, :].rearrange("p (u k s c) -> p u k s c", u=2, k=KC, s=SUB)
        vin = ring[:, :].rearrange("p (u r c) -> p u r c", u=4, r=R)
        qstage = stage[:, 0:2 * R * H].rearrange("p (u r c) -> p u r c", u=2, r=R)
        pstage = stage[:, 2 * R * H:2 * (R + RT) * H].rearrange("p (u r c) -> p u r c", u=2, r=RT)
        ystage = stage[:, 0:2 * TP].rearrange("p (u c) -> p u c", u=2)
        ytr = stage[:, 2 * TP:2 * TP + 2 * SUB * GC].rearrange("p (u s c) -> p u s c", u=2, s=SUB)
        assert 2 * TP + 2 * SUB * GC <= 2 * (R + RT) * H
        q_lines = qk[0:D, 0, :].rearrange("p (y x) -> p y x", x=W)
        k_lines = qk[0:D, 1, :].rearrange("p (y x) -> p y x", x=W)
        q_ori = [q_lines, q_lines.rearrange("p y x -> p x y")]
        k_ori = [k_lines, k_lines.rearrange("p y x -> p x y")]
        att4 = att[0:H, :, :].rearrange("p o (l i) -> p o l i", i=H)
        acc4 = qk[:, :, :].rearrange("p u (y x) -> p u y x", x=W)
        max_r, sum_r, max_c, sum_c, joint, fac_r, fac_ct, fac_c = (stat[0:H, i, :] for i in range(8))
        shifted = stat[0:H, 8:10, :]
        bias_qk, gam = cst[:, 0:1], cst[:, 1:2]

        pair = ctx.enter_context(nc.psum_tensor("pair", [P, 2, 2, 512], F32))
        bank = ctx.enter_context(nc.psum_tensor("bank", [P, 2, 512], F32))
        gram_ps = ctx.enter_context(nc.psum_tensor("gram_ps", [P, 512], F32))
        stat_ps = ctx.enter_context(nc.psum_tensor("stat_ps", [P, 512], F32))

        def lines(u, parts):
            return pair[0:parts, u, :, 0:4 * H].rearrange("p b (r i) -> p b r i", i=H)

        consts_loaded = sem("consts_loaded")
        consts_made = sem("consts_made")
        weights_scaled = sem("weights_scaled")
        x_loaded = [sem(f"x_loaded{u}") for u in range(2)]
        x_read = sem("x_read")
        pair_ready = sem("pair_ready")
        pair_free = sem("pair_free")
        bank_ready = sem("bank_ready")
        bank_free = sem("bank_free")
        v_stored = [sem(f"v_stored{u}") for u in range(2)]
        v_loaded = [sem(f"v_loaded{u}") for u in range(4)]
        q_staged = sem("q_staged")
        group_max = sem("group_max")
        exp_done = sem("exp_done")
        masked = sem("masked")
        sums_done = sem("sums_done")
        stat_t = sem("stat_t")
        shift_done = sem("shift_done")
        shift_exp = sem("shift_exp")
        chain = sem("chain")
        factors = sem("factors")
        ones_set = sem("ones_set")
        scaled = sem("scaled")
        acc_loaded = [sem(f"acc_loaded{u}") for u in range(2)]
        y_staged = sem("y_staged")
        y_stored = [sem(f"y_stored{u}") for u in range(2)]
        ytr_free = sem("ytr_free")
        gram_added = sem("gram_added")
        gram_out = sem("gram_out")
        gram_in = sem("gram_in")
        fact_made = sem("fact_made")
        fact_out = sem("fact_out")
        fact_in = sem("fact_in")
        sq_ready = sem("sq_ready")
        sq_done = sem("sq_done")
        wmat_zero = sem("wmat_zero")
        fy_loaded = [sem(f"fy_loaded{u}") for u in range(2)]
        fin_ready = [sem("fin_ready_act"), sem("fin_ready_dve")]
        fin_free = [sem("fin_free_act"), sem("fin_free_dve")]
        out_stored = [sem(f"out_stored{u}") for u in range(2)]

        FT = 2304
        FN = HW // FT
        FB = 384
        HFB = FT // FB // 2
        fy = att[:, 0, 0:2 * FT].rearrange("p (u c) -> p u c", u=2)
        fo = att[:, 1, 0:2 * FT].rearrange("p (u c) -> p u c", u=2)
        wmat = ring[:, 0:KC * P].rearrange("p (k c) -> p k c", k=KC)
        wbias = cst[:, 4:8]
        g_cov = qk[0:GROUPS, 0, 0:GS * GS].rearrange("p (i j) -> p i j", j=GS)
        g_sum = qk[0:GROUPS, 0, 256:256 + GS]
        g_mean = qk[0:GROUPS, 0, 272:272 + GS]
        g_tmp = qk[0:GROUPS, 0, 512:512 + GS * GS].rearrange("p (i j) -> p i j", j=GS)
        g_aug = qk[0:GROUPS, 0, 1024:1024 + 2 * GS * GS].rearrange("p (i j) -> p i j", j=2 * GS)
        g_fac = qk[0:GROUPS, 0, 2048:2048 + GS]
        g_piv = qk[0:GROUPS, 0, 2064:2064 + GS]
        g_rt = qk[0:GROUPS, 0, 2080:2080 + GS]
        g_bias = qk[0:GROUPS, 0, 2096:2096 + GS]
        g_rec = qk[0:GROUPS, 0, 2112:2113]
        g_wt = qk[0:GROUPS, 0, 2560:2560 + GS * GS].rearrange("p (j i) -> p j i", i=GS)
        g_eye = qk[0:GROUPS, 0, 3072:3072 + GS * GS].rearrange("p (i j) -> p i j", j=GS)

        block = ctx.enter_context(nc.Block())

        @block.sync
        def _(sp):
            sp.dma_start(wqk[:, :, 0:D], wq_t.rearrange("(k p) d -> p k d", p=P)).then_inc(consts_loaded, 16)
            sp.dma_start(wqk[:, :, D:2 * D], wk_t.rearrange("(k p) d -> p k d", p=P)).then_inc(consts_loaded, 16)
            sp.dma_start(wv[:, :, :], wv_t.rearrange("(k p) d -> p k d", p=P)).then_inc(consts_loaded, 16)
            sp.dma_start(cst[0:D, 0:1], bq.rearrange("(d a) -> d a", a=1)).then_inc(consts_loaded, 16)
            sp.dma_start(cst[D:2 * D, 0:1], bk.rearrange("(d a) -> d a", a=1)).then_inc(consts_loaded, 16)
            sp.dma_start(cst[:, 1:2], gamma.rearrange("(a b) -> a b", b=1).broadcast_to([P, 1])).then_inc(consts_loaded, 16)
            sp.dma_start(bv_rep[:, :], bv.rearrange("(a c) -> a c", a=1).broadcast_to([P, C])).then_inc(consts_loaded, 16)
            with sp.Fori(0, N) as n:
                with sp.Fori(0, NT // 2) as j:
                    for u in range(2):
                        sp.wait_ge(x_read, n * NT + j * 2 + u + 1)
                        sp.dma_start(xt[:, u, :, :], x_px[n, :, :, ds((j * 2 + u) * TP, TP)]).then_inc(x_loaded[u], 16)
                sp.wait_ge(v_stored[0], n * (8 * NT) + (8 * NT + 16))
                sp.wait_ge(v_stored[1], n * (8 * NT) + (8 * NT + 16))
                for cc in range(KC):
                    cu = cc % 2
                    if cc < 2:
                        sp.wait_ge(pair_ready, n * PAIR_READY + NT + 2 * NG)
                    else:
                        sp.wait_ge(y_staged, n * (KC * NT) + ((cc - 1) * NT + 1))
                        sp.wait_ge(y_stored[cu], (n * 2 + 2) * 16)
                    sp.dma_start(qk[:, cu, :], x_px[n, :, cc, :]).then_inc(acc_loaded[cu], 16)
                    with sp.Fori(0, NG // 4) as g:
                        for u in range(4):
                            sp.wait_ge(pair_ready, n * PAIR_READY + g * 4 + (NT + 2 * NG + cc * 2 * NG + u - 3))
                            sp.dma_start(vin[0:W, u, :, :], v_rows[n, cc, :, ds((g * 4 + u) * R, R), :]).then_inc(v_loaded[u], 16)
                    with sp.Fori(0, NG // 4) as g:
                        for u in range(4):
                            sp.wait_ge(pair_ready, n * PAIR_READY + g * 4 + (NT + 2 * NG + cc * 2 * NG + NG + u - 3))
                            sp.dma_start(vin[0:H, u, :, :], v_cols[n, cc, :, ds((g * 4 + u) * R, R), :]).then_inc(v_loaded[u], 16)
            sp.wait_ge(gram_added, N * KC + 1)
            sp.dma_start(gram_dram[:, :].rearrange("(k p) c -> p k c", p=P), gram_sb[:, :, :]).then_inc(gram_out, 16)
            sp.wait_ge(gram_out, 16)
            for u in range(2):
                sp.wait_ge(y_stored[u], N * 32 + 16)
            g_rows = gram_dram[:, :].rearrange("(k b i) c -> b k i c", k=KC, b=BPC)
            for b in range(BPC):
                sp.dma_start(g_cov[b:GROUPS:BPC, :, :], g_rows[b, :, :, b * GS:(b + 1) * GS]).then_inc(gram_in, 16)
                sp.dma_start(g_sum[b:GROUPS:BPC, :].unsqueeze(2), g_rows[b, :, :, P:P + 1], allow_slow_non_contiguous=True).then_inc(gram_in, 16)
            sp.wait_ge(fact_made, 1)
            sp.dma_start(wmat_dram[:, :, :], g_wt).then_inc(fact_out, 16)
            sp.dma_start(wbias_dram[:, :], g_bias).then_inc(fact_out, 16)
            sp.wait_ge(fact_out, 32)
            sp.wait_ge(wmat_zero, 1)
            for b in range(BPC):
                sp.dma_start(wmat[b * GS:(b + 1) * GS, :, b * GS:(b + 1) * GS],
                             wmat_dram[:, :, :].rearrange("(k b) j i -> b j k i", b=BPC)[b]).then_inc(fact_in, 16)
            sp.dma_start(wbias, wbias_dram[:, :].rearrange("(k b) i -> (b i) k", b=BPC), allow_slow_non_contiguous=True).then_inc(fact_in, 16)
            with sp.Fori(0, N) as n:
                for cc in range(KC):
                    for f in range(FN):
                        u = f % 2
                        sp.wait_ge(fin_ready[1], (n * (KC * FN) + (cc * FN + f + 1)) * HFB)
                        sp.dma_start(fy[:, u, :], y_dram[n, cc, :, f * FT:(f + 1) * FT]).then_inc(fy_loaded[u], 16)
            for u in range(2):
                sp.wait_ge(out_stored[u], 16 * N * KC * FN // 2 + 16)

        @block.gpsimd
        def _(pool):
            pool.sem_inc(y_staged, 1)
            pool.memset(ident[:, :], 1.0).then_inc(consts_made, 1)
            pool.memset(gram_sb[:, :, :], 0.0).then_inc(consts_made, 1)
            pool.memset(off_diag[:, :], 1.0).then_inc(consts_made, 1)
            pool.wait_ge(consts_made, 3)
            pool.affine_select(out=ident[:, :], in_=ident[:, :], compare_op=ALU.is_equal, fill=0.0, base=0,
                               pattern=[[-1, P]], channel_multiplier=1).then_inc(consts_made, 1)
            pool.affine_select(out=off_diag[:, :], in_=off_diag[:, :], compare_op=ALU.not_equal, fill=0.0, base=0,
                               pattern=[[-1, H]], channel_multiplier=1).then_inc(consts_made, 1)
            pool.wait_ge(consts_made, 5)
            with pool.Fori(0, N) as n:
                for o in range(2):
                    with pool.Fori(0, NG // 2) as g:
                        pool.wait_ge(bank_free, n * BANK_USES + 2 + NT)
                        for u in range(2):
                            pool.wait_ge(pair_ready, n * PAIR_READY + g * 2 + (NT + o * NG + u - 1))
                            pool.tensor_copy(qstage[0:D, u, :, :], q_ori[o][:, ds((g * 2 + u) * R, R), :]).then_inc(q_staged, 1)
                with pool.Fori(0, NG) as g:
                    pool.wait_ge(exp_done, n * 2 * NG + g + (NG + 1))
                    cols = att4[:, 1, ds(g * R, R), :]
                    pool.tensor_tensor(cols, cols, off_diag[:, :].unsqueeze(1).broadcast_to([H, R, H]), ALU.mult).then_inc(masked, 1)
                for o in range(2):
                    fac = fac_r if o == 0 else fac_c
                    with pool.Fori(0, NTR // 2) as g:
                        pool.wait_ge(factors, n + 1)
                        for u in range(2):
                            pool.wait_ge(bank_ready, n * BANK_USES + g * 2 + (NT + o * NTR + u - 1))
                            pool.tensor_tensor(pstage[0:H, u, :, :], att4[:, o, ds((g * 2 + u) * RT, RT), :],
                                               fac[:, ds((g * 2 + u) * RT, RT)].unsqueeze(2).broadcast_to([H, RT, H]),
                                               ALU.mult).then_inc(scaled, 1)
                for cc in range(KC):
                    with pool.Fori(0, NT // 2) as j:
                        pool.wait_ge(pair_free, n * PAIR_USES + (2 + 2 * NT + 2 * NG + (cc + 1) * 2 * NG))
                        for u in range(2):
                            pool.wait_ge(bank_ready, n * BANK_USES + j * 2 + (NT + 2 * NTR + cc * NT + u - 1))
                            pool.tensor_copy(ystage[:, u, :], qk[:, cc % 2, ds((j * 2 + u) * TP, TP)]).then_inc(y_staged, 1)

        @block.scalar
        def _(act):
            act.sem_inc(bank_free, 2)
            for u in range(2):
                act.sem_inc(v_stored[u], 16)
                act.sem_inc(y_stored[u], 16)
                act.sem_inc(out_stored[u], 16)
            act.sem_inc(fin_free[0], 2)
            act.wait_ge(consts_loaded, 7 * 16)
            with act.Fori(0, N) as n:
                act.wait_ge(y_stored[0], n * 32 + 16)
                act.wait_ge(y_stored[1], n * 32 + 16)
                act.wait_ge(y_staged, n * (KC * NT) + 1)
                with act.Fori(0, NT // 2) as j:
                    for u in range(2):
                        t = j * 2 + u
                        act.wait_ge(bank_ready, n * BANK_USES + t + 1)
                        nc.scalar.activation(qk[0:D, 0, ds(t * TP, TP)], bank[0:D, u, :], ACT.Identity, bias=cst[0:D, 0:1])
                        nc.scalar.activation(qk[0:D, 1, ds(t * TP, TP)], bank[D:2 * D, u, :], ACT.Identity,
                                             bias=cst[D:2 * D, 0:1]).then_inc(bank_free, 1)
                        act.wait_ge(pair_free, n * PAIR_USES + t * 2 + 4)
                        act.dma_start(v_tile[n, ds(t * P, P), :, :],
                                      vout[:, u, :, :, :].rearrange("p k s c -> p k (s c)")).then_inc(v_stored[u], 16)
                with act.Fori(0, 2 * NG) as g:
                    act.wait_ge(pair_free, n * PAIR_USES + g + (2 * NT + 3))
                    flat = att[0:H, :, :].rearrange("p o i -> p (o i)")[:, ds(g * R * H, R * H)]
                    nc.scalar.activation(flat, flat, ACT.Exp).then_inc(exp_done, 1)
                act.wait_ge(shift_done, n * 2 + 2)
                nc.scalar.activation(shifted, shifted, ACT.Exp).then_inc(shift_exp, 1)
                att_flat = att[0:H, :, :].rearrange("p o i -> p (o i)")
                with act.Fori(0, NTR) as g:
                    for u in range(2):
                        act.wait_ge(bank_ready, n * BANK_USES + g * 2 + (NT + u + 1))
                        nc.scalar.copy(att_flat[:, ds((g * 2 + u) * RT * H, RT * H)], bank[0:H, u, 0:RT * H]).then_inc(bank_free, 1)
                act.wait_ge(ones_set, n + 1)
                for cc in range(KC):
                    act.wait_ge(pair_free, n * PAIR_USES + (2 + 2 * NT + 2 * NG + (cc + 1) * 2 * NG))
                    act.dma_start(y_dram[n, cc, :, :], qk[:, cc % 2, :]).then_inc(y_stored[cc % 2], 16)
                    with act.Fori(0, NT // 2) as j:
                        for u in range(2):
                            act.wait_ge(bank_ready, n * BANK_USES + j * 2 + (NT + 2 * NTR + cc * NT + u + 1))
                            act.wait_ge(ytr_free, n * (KC * NT) + cc * NT + j * 2 + u + 1)
                            nc.scalar.copy(ytr[:, u, :, 0:P], bank[:, u, :].rearrange("p (s c) -> p s c", c=P)).then_inc(bank_free, 1)
            act.wait_ge(sq_ready, 1)
            nc.scalar.activation(g_rt, g_piv, ACT.Sqrt).then_inc(sq_done, 1)
            act.wait_ge(fact_in, 16 * (BPC + 1))
            with act.Fori(0, N) as n:
                for cc in range(KC):
                    for f in range(FN):
                        u = f % 2
                        act.wait_ge(out_stored[u], (n * (KC * FN // 2) + (cc * FN // 2 + f // 2 + 1)) * 16)
                        for b in range(HFB):
                            act.wait_ge(fin_ready[0], n * (KC * FN * HFB) + ((cc * FN + f) * HFB + b + 1))
                            nc.scalar.activation(fo[:, u, 2 * b * FB:(2 * b + 1) * FB], bank[:, (f * HFB + b) % 2, 0:FB],
                                                 ACT.Identity, bias=wbias[:, cc:cc + 1]).then_inc(fin_free[0], 1)
                        for e in range(2):
                            act.wait_ge(fin_free[e], n * (KC * FN * HFB) + ((cc * FN + f + 1) * HFB + 2))
                        act.dma_start(out_px[n, cc, :, f * FT:(f + 1) * FT],
                                      fo[:, u, :]).then_inc(out_stored[u], 16)

        @block.vector
        def _(dve):
            nc.vector.sem_inc(pair_free, 2)
            nc.vector.sem_inc(gram_added, 1)
            nc.vector.sem_inc(fin_free[1], 2)
            steps = [0]

            def link(ins):
                steps[0] += 1
                ins.then_inc(chain, 1)
                dve.wait_ge(chain, steps[0])

            dve.wait_ge(consts_loaded, 7 * 16)
            nc.vector.tensor_scalar(wv[:, :, :], wv[:, :, :], gam, None, ALU.mult).then_inc(weights_scaled, 1)
            link(nc.vector.tensor_scalar(bv_rep[:, :], bv_rep[:, :], gam, None, ALU.mult))
            dve.wait_ge(consts_made, 5)
            
            with dve.Fori(0, N) as n:
                with dve.Fori(0, NT // 2) as j:
                    for u in range(2):
                        t = j * 2 + u
                        dve.wait_ge(v_stored[u], (n * (NT // 2) + j + 1) * 16)
                        for h in range(2):
                            if h == 0:
                                dve.wait_ge(pair_ready, n * PAIR_READY + t + 1)
                            else:
                                dve.wait_ge(x_read, n * NT + t + 3)
                            nc.vector.tensor_tensor(
                                vout[:, u, :, 2 * h:2 * h + 2, :].rearrange("p k s c -> p s k c"),
                                pair[:, h, :, :].rearrange("p s (k c) -> p s k c", c=P),
                                bv_rep[:, :].rearrange("p (a k c) -> p a k c", a=1, c=P).broadcast_to([P, 2, KC, P]),
                                ALU.add).then_inc(pair_free, 1)
                for o in range(2):
                    mx = max_r if o == 0 else max_c
                    with dve.Fori(0, NG // 2) as g:
                        for u in range(2):
                            l = (g * 2 + u) * R
                            dve.wait_ge(pair_ready, n * PAIR_READY + g * 2 + (NT + o * NG + u + 1))
                            nc.vector.tensor_reduce(mx[:, ds(l, R)].rearrange("p (b r) -> p b r", b=2), lines(u, H), AX.X, ALU.max).then_inc(group_max, 1)
                            dve.wait_ge(group_max, n * 2 * NG + g * 2 + (o * NG + u + 1))
                            for b in range(2):
                                last = nc.vector.tensor_tensor(
                                    att4[:, o, ds(l + b * 4, 4), :], lines(u, H)[:, b],
                                    mx[:, ds(l + b * 4, 4)].unsqueeze(2).broadcast_to([H, 4, H]), ALU.subtract)
                            last.then_inc(pair_free, 1)
                for o in range(2):
                    sm = sum_r if o == 0 else sum_c
                    with dve.Fori(0, NG) as g:
                        if o == 0:
                            dve.wait_ge(exp_done, n * 2 * NG + g + 1)
                        else:
                            dve.wait_ge(masked, n * NG + g + 1)
                        nc.vector.tensor_reduce(sm[:, ds(g * R, R)], att4[:, o, ds(g * R, R), :], AX.X, ALU.add).then_inc(sums_done, 1)
                def stage_link(k, ins):
                    ins.then_inc(chain, 1)
                    dve.wait_ge(chain, n * SMALL + (1 + k))
                dve.wait_ge(stat_t, n * 2 + 1)
                max_ct, sum_ct, fac_ps = (stat_ps[0:H, i * H:(i + 1) * H] for i in range(3))
                stage_link(1, nc.vector.tensor_tensor(joint, max_r, max_ct, ALU.max))
                nc.vector.tensor_tensor(shifted[:, 0, :], max_r, joint, ALU.subtract).then_inc(shift_done, 1)
                nc.vector.tensor_tensor(shifted[:, 1, :], max_ct, joint, ALU.subtract).then_inc(shift_done, 1)
                dve.wait_ge(shift_exp, n + 1)
                nc.vector.tensor_tensor(fac_r, sum_r, shifted[:, 0, :], ALU.mult).then_inc(chain, 1)
                stage_link(3, nc.vector.tensor_tensor(fac_ct, sum_ct, shifted[:, 1, :], ALU.mult))
                stage_link(4, nc.vector.tensor_tensor(joint, fac_r, fac_ct, ALU.add))
                stage_link(5, nc.vector.reciprocal(joint, joint))
                stage_link(6, nc.vector.tensor_tensor(fac_ct, shifted[:, 1, :], joint, ALU.mult))
                stage_link(7, nc.vector.tensor_tensor(fac_r, shifted[:, 0, :], joint, ALU.mult))
                dve.wait_ge(stat_t, n * 2 + 2)
                nc.vector.tensor_copy(fac_c, fac_ps).then_inc(factors, 1)
                dve.wait_ge(bank_ready, n * BANK_USES + (NT + 2 * NTR))
                nc.vector.memset(ytr[:, :, :, P:GC], 1.0).then_inc(ones_set, 1)
                for cc in range(KC):
                    cu = cc % 2
                    for o in range(2):
                        with dve.Fori(0, NG // 2) as g:
                            if o == 0:
                                dve.wait_ge(acc_loaded[cu], (n * 2 + cc // 2 + 1) * 16)
                            else:
                                dve.wait_ge(pair_free, n * PAIR_USES + (2 + 2 * NT + 2 * NG + (2 * cc + 1) * NG))
                            for u in range(2):
                                dve.wait_ge(pair_ready, n * PAIR_READY + g * 2 + (NT + 2 * NG + (2 * cc + o) * NG + u + 1))
                                l = (g * 2 + u) * R
                                if o == 0:
                                    dst = qk[:, cu, ds(l * W, R * W)].rearrange("p (b i) -> p b i", b=2)
                                    src = pair[:, u, :, 0:4 * W]
                                    nc.vector.tensor_tensor(dst, src, dst, ALU.add).then_inc(pair_free, 1)
                                else:
                                    dst = acc4[:, cu, :, ds(l, R)].rearrange("p y (b r) -> p b r y", b=2)
                                    nc.vector.tensor_tensor(dst, lines(u, P), dst, ALU.add).then_inc(pair_free, 1)
                    dve.wait_ge(ytr_free, n * (KC * NT) + cc * NT + (NT + 2))
                    nc.vector.tensor_tensor(gram_sb[:, cc, :], gram_ps[:, 0:GC], gram_sb[:, cc, :], ALU.add).then_inc(gram_added, 1)
            steps[0] = 1 + N * SMALL
            INV = 1.0 / (N * HW)
            dve.wait_ge(gram_in, 32 * BPC)
            link(nc.vector.tensor_scalar(g_mean, g_sum, INV, None, ALU.mult))
            link(nc.vector.tensor_tensor(g_tmp, g_mean.unsqueeze(2).broadcast_to([GROUPS, GS, GS]),
                                         g_mean.unsqueeze(1).broadcast_to([GROUPS, GS, GS]), ALU.mult))
            link(nc.vector.tensor_scalar(g_cov, g_cov, INV, None, ALU.mult))
            link(nc.vector.tensor_tensor(g_cov, g_cov, g_tmp, ALU.subtract))
            link(nc.vector.memset(g_eye, 0.0))
            link(nc.vector.memset(qk[0:GROUPS, 0, 3072:3072 + GS * GS:GS + 1], 1.0))
            link(nc.vector.tensor_scalar(g_aug[:, :, 0:GS], g_cov, 1.0 - EPS, None, ALU.mult))
            link(nc.vector.tensor_scalar(g_tmp, g_eye, EPS, None, ALU.mult))
            link(nc.vector.tensor_tensor(g_aug[:, :, 0:GS], g_aug[:, :, 0:GS], g_tmp, ALU.add))
            link(nc.vector.tensor_copy(g_aug[:, :, GS:2 * GS], g_eye))
            for k in range(GS - 1):
                m = GS - 1 - k
                link(nc.vector.reciprocal(g_rec, g_aug[:, k, k:k + 1]))
                link(nc.vector.tensor_scalar(g_fac[:, 0:m].unsqueeze(2), g_aug[:, k + 1:GS, k:k + 1], g_rec, None, ALU.mult))
                link(nc.vector.tensor_tensor(g_tmp[:, 0:m, :], g_fac[:, 0:m].unsqueeze(2).broadcast_to([GROUPS, m, GS]),
                                             g_aug[:, k, k + 1:k + 1 + GS].unsqueeze(1).broadcast_to([GROUPS, m, GS]), ALU.mult))
                link(nc.vector.tensor_tensor(g_aug[:, k + 1:GS, k + 1:k + 1 + GS], g_aug[:, k + 1:GS, k + 1:k + 1 + GS],
                                             g_tmp[:, 0:m, :], ALU.subtract))
            nc.vector.tensor_copy(g_piv, qk[0:GROUPS, 0, 1024:1024 + 2 * GS * GS:2 * GS + 1]).then_inc(sq_ready, 1)
            dve.wait_ge(sq_done, 1)
            link(nc.vector.reciprocal(g_piv, g_rt))
            link(nc.vector.tensor_tensor(g_wt, g_aug[:, :, GS:2 * GS].rearrange("p i j -> p j i"),
                                         g_piv.unsqueeze(1).broadcast_to([GROUPS, GS, GS]), ALU.mult))
            link(nc.vector.tensor_tensor(g_tmp, g_wt.rearrange("p j i -> p i j"),
                                         g_mean.unsqueeze(1).broadcast_to([GROUPS, GS, GS]), ALU.mult))
            nc.vector.tensor_reduce(g_bias, g_tmp, AX.X, ALU.add, negate=True).then_inc(fact_made, 1)
            nc.vector.memset(wmat, 0.0).then_inc(wmat_zero, 1)
            dve.wait_ge(fact_in, 16 * (BPC + 1))
            with dve.Fori(0, N) as n:
                for cc in range(KC):
                    for f in range(FN):
                        u = f % 2
                        dve.wait_ge(out_stored[u], (n * (KC * FN // 2) + (cc * FN // 2 + f // 2 + 1)) * 16)
                        for b in range(HFB):
                            dve.wait_ge(fin_ready[1], n * (KC * FN * HFB) + ((cc * FN + f + 2) * HFB + b + 1))
                            nc.vector.tensor_scalar(fo[:, u, (2 * b + 1) * FB:(2 * b + 2) * FB],
                                                    pair[:, (f * HFB + b) % 2, 0, 0:FB],
                                                    wbias[:, cc:cc + 1], None, ALU.add).then_inc(fin_free[1], 1)

        @block.tensor
        def _(pe):
            pe.sem_inc(x_read, 2)
            pe.sem_inc(ytr_free, 2)
            pe.wait_ge(consts_loaded, 7 * 16)
            pe.wait_ge(weights_scaled, 1)
            pe.wait_ge(consts_made, 5)

            with pe.Fori(0, N) as n:
                with pe.Fori(0, NT // 2) as j:
                    for u in range(2):
                        t = j * 2 + u
                        pe.wait_ge(x_loaded[u], (n * (NT // 2) + j + 1) * 16)
                        pe.wait_ge(bank_free, n * BANK_USES + t + 1)
                        for k in range(KC):
                            last = nc.tensor.matmul(bank[:, u, :], wqk[:, k, :], xt[:, u, k, :], start=k == 0, stop=k == KC - 1)
                        last.then_inc(bank_ready, 1)
                        for h in range(2):
                            pe.wait_ge(pair_free, n * PAIR_USES + t * 2 + h + 1)
                            for s in range(2):
                                for k in range(KC):
                                    last = nc.tensor.matmul(pair[:, h, s, :], xt[:, u, k, 2 * h + s::SUB], wv[:, k, :],
                                                            start=k == 0, stop=k == KC - 1)
                            last.then_inc(pair_ready if h == 0 else x_read, 1)
                for o in range(2):
                    with pe.Fori(0, NG // 2) as g:
                        for u in range(2):
                            pe.wait_ge(q_staged, n * 2 * NG + g * 2 + (o * NG + u + 1))
                            pe.wait_ge(pair_free, n * PAIR_USES + g * 2 + (2 * NT + o * NG + u + 1))
                            for r in range(R):
                                last = nc.tensor.matmul(lines(u, H)[:, r // 4, r % 4, :], qstage[0:D, u, r, :],
                                                        k_ori[o][:, (g * 2 + u) * R + r, :],
                                                        start=True, stop=True)
                            last.then_inc(pair_ready, 1)
                pe.wait_ge(sums_done, (n + 1) * 2 * NG)
                nc.tensor.transpose(stat_ps[0:H, 0:H], max_c, ident[0:H, 0:H])
                nc.tensor.transpose(stat_ps[0:H, H:2 * H], sum_c, ident[0:H, 0:H]).then_inc(stat_t, 1)
                pe.wait_ge(chain, n * SMALL + 1 + 6)
                nc.tensor.transpose(stat_ps[0:H, 2 * H:3 * H], fac_ct, ident[0:H, 0:H]).then_inc(stat_t, 1)
                with pe.Fori(0, NTR) as g:
                    for u in range(2):
                        pe.wait_ge(scaled, n * 2 * NTR + g * 2 + (u + 1))
                        pe.wait_ge(bank_free, n * BANK_USES + g * 2 + (NT + u + 1))
                        for r in range(RT):
                            last = nc.tensor.transpose(bank[0:H, u, r * H:(r + 1) * H], pstage[0:H, u, r, :], ident[0:H, 0:H])
                        last.then_inc(bank_ready, 1)
                for cc in range(KC):
                    for o in range(2):
                        with pe.Fori(0, NG // 4) as g:
                            if cc == 0:
                                pe.wait_ge(bank_free, n * BANK_USES + (NT + 2 * NTR + 2))
                            for v in range(4):
                                u = v % 2
                                pe.wait_ge(v_loaded[v], n * (KC * 2 * (NG // 4) * 16) + g * 16 + ((2 * cc + o) * (NG // 4) + 1) * 16)
                                pe.wait_ge(pair_free, n * PAIR_USES + g * 4 + (2 * NT + 2 * NG + (2 * cc + o) * NG + v + 1))
                                for r in range(R):
                                    last = nc.tensor.matmul(lines(u, P)[:, r // 4, r % 4, :], vin[0:H, v, r, :],
                                                            att4[:, o, (g * 4 + v) * R + r, :],
                                                            start=True, stop=True)
                                last.then_inc(pair_ready, 1)

                    def turn(b, j=0):
                        u = b % 2
                        pe.wait_ge(y_staged, n * (KC * NT) + j * 2 + (cc * NT + b + 2))
                        pe.wait_ge(bank_free, n * BANK_USES + j * 2 + (NT + 2 * NTR + cc * NT + b + 1))
                        for s in range(SUB):
                            last = nc.tensor.transpose(bank[:, u, s * P:(s + 1) * P], ystage[:, u, s * P:(s + 1) * P], ident[:, :])
                        last.then_inc(bank_ready, 1)

                    def products(b, j=0, first=False, final=False):
                        u = b % 2
                        pe.wait_ge(bank_free, n * BANK_USES + j * 2 + (NT + 2 * NTR + cc * NT + b + 3))
                        for s in range(SUB):
                            last = nc.tensor.matmul(gram_ps[:, 0:GC], ytr[:, u, s, 0:P], ytr[:, u, s, :],
                                                    start=first and s == 0, stop=final and s == SUB - 1)
                        last.then_inc(ytr_free, 1)

                    turn(0)
                    turn(1)
                    pe.wait_ge(gram_added, n * KC + (cc + 1))
                    products(0, first=True)
                    with pe.Fori(0, NT // 2 - 1) as j:
                        turn(2, j)
                        products(1, j)
                        turn(3, j)
                        products(2, j)
                    products(NT - 1, final=True)
            pe.sem_inc(fin_ready[1], 2 * HFB)
            pe.wait_ge(fact_in, 16 * (BPC + 1))
            with pe.Fori(0, N) as n:
                for cc in range(KC):
                    for f in range(FN):
                        u = f % 2
                        pe.wait_ge(fy_loaded[u], (n * (KC * FN // 2) + (cc * FN // 2 + f // 2 + 1)) * 16)
                        for b in range(HFB):
                            for e, dst in enumerate((bank[:, (f * HFB + b) % 2, 0:FB], pair[:, (f * HFB + b) % 2, 0, 0:FB])):
                                pe.wait_ge(fin_free[e], n * (KC * FN * HFB) + ((cc * FN + f) * HFB + b + 1))
                                nc.tensor.matmul(dst, wmat[:, cc, :], fy[:, u, (2 * b + e) * FB:(2 * b + e + 1) * FB],
                                                 start=True, stop=True).then_inc(fin_ready[e], 1)


def kernel(**inputs):
    import concourse.bacc as bacc
    from concourse.bass_utils import run_bass_kernel_spmd

    nc = bacc.Bacc("TRN2", target_bir_lowering=False, num_devices=1)
    arrays = {
        "x": np.ascontiguousarray(inputs["x"]),
        "wq_t": np.ascontiguousarray(np.asarray(inputs["L0_conv_wq"]).T),
        "bq": np.ascontiguousarray(inputs["L0_conv_bq"]),
        "wk_t": np.ascontiguousarray(np.asarray(inputs["L0_conv_wk"]).T),
        "bk": np.ascontiguousarray(inputs["L0_conv_bk"]),
        "wv_t": np.ascontiguousarray(np.asarray(inputs["L0_conv_wv"]).T),
        "bv": np.ascontiguousarray(inputs["L0_conv_bv"]),
        "gamma": np.asarray(inputs["L0_conv_gamma"]).reshape(1),
    }
    args = [nc.dram_tensor(name, a.shape, mybir.dt.from_np(a.dtype), kind="ExternalInput").ap()
            for name, a in arrays.items()]
    out = nc.dram_tensor("out", arrays["x"].shape, mybir.dt.float32, kind="ExternalOutput")
    criss_cross_whitening_kernel(nc, *args, out.ap())
    result = run_bass_kernel_spmd(nc, [arrays], core_ids=[0])
    return result.results[0]["out"]
```

```python
from contextlib import ExitStack

import numpy as np

import concourse.bass as bass
from concourse import mybir


def criss_cross_whitening_kernel(nc, x, wq_t, bq, wk_t, bk, wv_t, bv, gamma, out):
    F32 = mybir.dt.float32
    F16 = mybir.dt.float16
    F32R = mybir.dt.float32r
    ALU = mybir.AluOpType
    ACT = mybir.ActivationFunctionType
    AX = mybir.AxisListType
    ds = bass.ds

    N, C, H, W = x.shape
    P = 128
    HW = H * W
    D = wq_t.shape[1]
    KC = C // P
    TP = 256
    NT = HW // TP
    SUB = TP // P
    TQ = 512
    NQ = HW // TQ
    QS = 6
    R = 8
    NG = H // R
    RT = 4
    NTR = 2 * H // RT
    TB = 512
    NB = HW // TB
    SB = TB // P
    GS, EPS = 16, 0.001
    GROUPS = C // GS
    BPC = P // GS
    GC = 2 * P + 2
    HALF_TOP = 2.0 ** 15
    ATT_UP = 2.0 ** 14
    assert NQ % QS == 0 and NB % 3 == 0 and NG % 3 == 0
    assert H == W and NT % 6 == 0 and NB % 2 == 0 and NG % 4 == 0 and H % R == 0 and KC % 2 == 0

    PAIR_V = 2 * NG
    PAIR_A = PAIR_V + NT
    PAIR_USES = PAIR_A + KC * 2 * NG
    READY_A = 2 * NG
    PAIR_READY = READY_A + KC * 2 * NG
    BANK_G = NTR
    BANK_USES = BANK_G + KC * NB
    UNITS = SUB * NT
    D_STAT = 8
    D_FAC = 10
    D_TURN = 12
    TPT = NTR // (NT - D_TURN)
    SUMS = 2 * NG // D_STAT
    PIECE = 2 * HW // (NT - D_TURN)
    HALF_LOADS = HW // PIECE + 2 * NG // 4
    Y_PIECE = 3 * TB
    Y_STORES = 2 * HW // Y_PIECE
    BIASED = 2 * HW // PIECE + KC - 2
    SMALL = 6
    CHAIN0 = 3
    BOUNDS = 9
    assert TPT == 2 and SUMS * D_STAT == 2 * NG and HW % PIECE == 0

    x_px = x.rearrange("n (k p) h w -> n p k (h w)", p=P)
    out_px = out.rearrange("n (k p) h w -> n k p (h w)", p=P)
    v_dram = nc.dram_tensor("v_dram", [N, KC, HW, 2, P], F16)
    y_dram = nc.dram_tensor("y_dram", [N, KC, P, HW], F32)
    v_rows = v_dram[:, :, :, :, :].rearrange("n k (y x) h c -> n k x y (h c)", x=W)
    v_cols = v_dram[:, :, :, :, :].rearrange("n k (y x) h c -> n k y x (h c)", x=W)
    v_tile = v_dram[:, :, :, :, :].rearrange("n k (q s) h c -> n q k (s h c)", s=SUB)
    gram_dram = nc.dram_tensor("gram_dram", [C, GC], F32)
    wmat_dram = nc.dram_tensor("wmat_dram", [GROUPS, GS, GS], F32)
    wbias_dram = nc.dram_tensor("wbias_dram", [GROUPS, GS], F32)

    ctx = ExitStack()
    with ctx:
        def sb(name, shape):
            return ctx.enter_context(nc.sbuf_tensor(name, shape, F32))

        def sem(name):
            return ctx.enter_context(nc.semaphore(name))

        qk = sb("qk", [P, 2, HW])
        att = sb("att", [P, 2, HW])
        wqk = sb("wqk", [P, KC, 2 * D])
        wv_hi = ctx.enter_context(nc.sbuf_tensor("wv_hi", [P, KC, C], F32R))
        wv_lo = ctx.enter_context(nc.sbuf_tensor("wv_lo", [P, KC, C], F32R))
        xt = sb("xt", [P, 2, KC, TP])
        xs = ctx.enter_context(nc.sbuf_tensor("xs", [P, 2, 2, KC, P], F32R))
        vbuf = ctx.enter_context(nc.sbuf_tensor("vbuf", [P, 2 * R * 2 * P], F16))
        ytr = ctx.enter_context(nc.sbuf_tensor("ytr", [P, 2, SB, GC], F16))
        pbuf = sb("pbuf", [P, 2 * RT * H])
        pstage = pbuf[0:H, :].rearrange("p (v r i) -> p v r i", v=2, r=RT)
        ytr_slots = [ytr[:, 0, :, :], ytr[:, 1, :, :],
                     pbuf[:, :].bitcast(F16)[:, 0:SB * GC].rearrange("p (s c) -> p s c", s=SB)]
        xmax = sb("xmax", [P, NQ])
        ones_row = sb("ones_row", [1, P])
        ident = sb("ident", [P, P])
        off_diag = sb("off_diag", [H, H])
        stat = sb("stat", [P, 10, H])
        gram_sb = sb("gram_sb", [P, KC, GC])
        cst = sb("cst", [P, 24])

        vout = vbuf[:, :].rearrange("p (u k s h c) -> p u k s h c", u=2, k=KC, s=SUB, h=2)
        xs_halves = xs[:, :, :, :, :].bitcast(F16).rearrange("p u h k c -> p u (h k c)")
        vin = [xs_halves[:, u, :].rearrange("p (r c) -> p r c", r=R) for u in range(2)]
        vin += [vbuf[:, u * R * 2 * P:(u + 1) * R * 2 * P].rearrange("p (r c) -> p r c", r=R) for u in range(2)]
        xq = att[:, :, :].rearrange("p o i -> p (o i)")[:, 0:QS * KC * TQ].rearrange("p (u k t) -> p u k t", u=QS, k=KC)
        wv_raw = qk[:, 0, 0:KC * C].rearrange("p (k c) -> p k c", k=KC)
        wv_gam = qk[:, 1, 0:KC * C].rearrange("p (k c) -> p k c", k=KC)
        wv_abs = qk[:, 0, KC * C:2 * KC * C].rearrange("p (k c) -> p k c", k=KC)
        ones_sq = qk[:, 1, KC * C:KC * C + P]
        bv_rep = qk[:, 1, KC * C + P:KC * C + P + C]
        q_lines = qk[0:D, 0, :].rearrange("p (y x) -> p y x", x=W)
        k_lines = qk[0:D, 1, :].rearrange("p (y x) -> p y x", x=W)
        q_ori = [q_lines, q_lines.rearrange("p y x -> p x y")]
        k_ori = [k_lines, k_lines.rearrange("p y x -> p x y")]
        att_lines = att[0:H, :, :].rearrange("p o (l i) -> p (o l) i", i=H)
        att_parts = att[0:H, :, :].bitcast(F16).rearrange("p o (l h i) -> p (o l) h i", h=2, i=H)
        att4 = att[0:H, :, :].rearrange("p o (l i) -> p o l i", i=H)
        qk_flat = qk[:, :, :].rearrange("p u i -> p (u i)")
        acc4 = qk[:, :, :].rearrange("p u (y x) -> p u y x", x=W)
        max_r, sum_r, max_c, sum_c, joint, fac_ct, fac_r, fac_c = (stat[0:H, i, :] for i in range(8))
        factor = stat[0:H, 6:8, :].rearrange("p o l -> p (o l)")
        shifted = stat[0:H, 8:10, :]
        bias_qk, gam = cst[:, 0:1], cst[:, 1:2]
        w_norm, bv_top = cst[:, 2:3], cst[:, 3:4]
        out_bias = cst[:, 8:12]
        v_up, v_down, y_up, y_down, y_down2, x_top, v_top, y_top, x_col = (cst[:, i:i + 1] for i in range(12, 21))

        pair = ctx.enter_context(nc.psum_tensor("pair", [P, 2, 2, 512], F32))
        bank = ctx.enter_context(nc.psum_tensor("bank", [P, 2, 512], F32))
        gram_ps = ctx.enter_context(nc.psum_tensor("gram_ps", [P, 512], F32))
        stat_ps = ctx.enter_context(nc.psum_tensor("stat_ps", [P, 512], F32))

        agg_ps = [pair[:, 0, :, :], pair[:, 1, :, :], bank[:, :, :]]
        turn_ps = [bank[:, 0, :], bank[:, 1, :], stat_ps[:, :]]

        def lines(u, parts):
            return pair[0:parts, u, :, 0:4 * H].rearrange("p b (r i) -> p b r i", i=H)

        def agg_lines(v):
            return agg_ps[v][:, :, 0:4 * H].rearrange("p b (r i) -> p b r i", i=H)

        consts_loaded = sem("consts_loaded")
        consts_made = sem("consts_made")
        weights_scaled = sem("weights_scaled")
        weights_hi = sem("weights_hi")
        weights_lo = sem("weights_lo")
        x_loaded = [sem(f"x_loaded{u}") for u in range(2)]
        xq_loaded = [sem(f"xq_loaded{u}") for u in range(QS)]
        xs_hi = sem("xs_hi")
        xs_lo = sem("xs_lo")
        unit_read = sem("unit_read")
        pair_ready = sem("pair_ready")
        pair_free = sem("pair_free")
        qk_ready = sem("qk_ready")
        qk_free = sem("qk_free")
        bank_ready = sem("bank_ready")
        bank_high = sem("bank_high")
        bank_free = sem("bank_free")
        v_high = sem("v_high")
        x_seen = sem("x_seen")
        norm_ready = sem("norm_ready")
        weights_abs = sem("weights_abs")
        bound_t = sem("bound_t")
        bound_m = sem("bound_m")
        bounds_done = sem("bounds_done")
        biased = sem("biased")
        v_stored = [sem(f"v_stored{u}") for u in range(2)]
        v_loaded = [sem(f"v_loaded{u}") for u in range(4)]
        group_max = sem("group_max")
        exp_done = sem("exp_done")
        masked = sem("masked")
        sums_done = sem("sums_done")
        stat_t = sem("stat_t")
        shift_done = sem("shift_done")
        shift_exp = sem("shift_exp")
        chain = sem("chain")
        factors = sem("factors")
        staged = sem("staged")
        acc_loaded = [sem(f"acc_loaded{u}") for u in range(2)]
        y_stored = [sem(f"y_stored{u}") for u in range(2)]
        ytr_free = sem("ytr_free")
        gram_added = sem("gram_added")
        gram_out = sem("gram_out")
        gram_in = sem("gram_in")
        fact_made = sem("fact_made")
        fact_out = sem("fact_out")
        fact_in = sem("fact_in")
        sq_ready = sem("sq_ready")
        sq_done = sem("sq_done")
        wmat_zero = sem("wmat_zero")
        fy_loaded = [sem(f"fy_loaded{u}") for u in range(2)]
        fin_ready = [sem("fin_ready_act"), sem("fin_ready_dve")]
        fin_free = [sem("fin_free_act"), sem("fin_free_dve")]
        out_stored = [sem(f"out_stored{u}") for u in range(2)]

        FT = 2304
        FN = HW // FT
        FB = 384
        HFB = FT // FB // 2
        fy = att[:, 0, 0:2 * FT].rearrange("p (u c) -> p u c", u=2)
        fo = att[:, 1, 0:2 * FT].rearrange("p (u c) -> p u c", u=2)
        wmat = vbuf[:, :].bitcast(F32)[:, 0:KC * P].rearrange("p (k c) -> p k c", k=KC)
        wbias = cst[:, 4:8]
        g_cov = qk[0:GROUPS, 0, 0:GS * GS].rearrange("p (i j) -> p i j", j=GS)
        g_sum = qk[0:GROUPS, 0, 256:256 + GS]
        g_mean = qk[0:GROUPS, 0, 272:272 + GS]
        g_tmp = qk[0:GROUPS, 0, 512:512 + GS * GS].rearrange("p (i j) -> p i j", j=GS)
        g_aug = qk[0:GROUPS, 0, 1024:1024 + 2 * GS * GS].rearrange("p (i j) -> p i j", j=2 * GS)
        g_fac = qk[0:GROUPS, 0, 2048:2048 + GS]
        g_piv = qk[0:GROUPS, 0, 2064:2064 + GS]
        g_rt = qk[0:GROUPS, 0, 2080:2080 + GS]
        g_bias = qk[0:GROUPS, 0, 2096:2096 + GS]
        g_rec = qk[0:GROUPS, 0, 2112:2113]
        g_low = qk[0:GROUPS, 0, 3584:3584 + GS * GS].rearrange("p (i j) -> p i j", j=GS)
        g_wt = qk[0:GROUPS, 0, 2560:2560 + GS * GS].rearrange("p (j i) -> p j i", i=GS)
        g_eye = qk[0:GROUPS, 0, 3072:3072 + GS * GS].rearrange("p (i j) -> p i j", j=GS)

        block = ctx.enter_context(nc.Block())

        @block.sync
        def _(sp):
            sp.dma_start(wqk[:, :, 0:D], wq_t.rearrange("(k p) d -> p k d", p=P)).then_inc(consts_loaded, 16)
            sp.dma_start(wqk[:, :, D:2 * D], wk_t.rearrange("(k p) d -> p k d", p=P)).then_inc(consts_loaded, 16)
            sp.dma_start(wv_raw, wv_t.rearrange("(k p) d -> p k d", p=P)).then_inc(consts_loaded, 16)
            sp.dma_start(cst[0:D, 0:1], bq.rearrange("(d a) -> d a", a=1)).then_inc(consts_loaded, 16)
            sp.dma_start(cst[D:2 * D, 0:1], bk.rearrange("(d a) -> d a", a=1)).then_inc(consts_loaded, 16)
            sp.dma_start(cst[:, 1:2], gamma.rearrange("(a b) -> a b", b=1).broadcast_to([P, 1])).then_inc(consts_loaded, 16)
            sp.dma_start(out_bias, bv.rearrange("(k p) -> p k", p=P), allow_slow_non_contiguous=True).then_inc(consts_loaded, 16)
            sp.dma_start(bv_rep, bv.rearrange("(a c) -> a c", a=1).broadcast_to([P, C])).then_inc(consts_loaded, 16)

            with sp.Fori(0, N) as n:
                def load_x(t, u):
                    sp.dma_start(xt[:, u, :, :], x_px[n, :, :, ds(t * TP, TP)]).then_inc(x_loaded[u], 16)

                for u in range(QS):
                    sp.wait_ge(pair_free, n * PAIR_USES + 2)
                    sp.dma_start(xq[:, u, :, :], x_px[n, :, :, u * TQ:(u + 1) * TQ]).then_inc(xq_loaded[u], 16)
                with sp.Fori(1, NQ // QS) as j:
                    for u in range(QS):
                        sp.wait_ge(x_seen, n * NQ + j * QS + (u + 1 - QS))
                        sp.wait_ge(qk_ready, n * NQ + j * QS + (u + 1 - QS))
                        sp.dma_start(xq[:, u, :, :], x_px[n, :, :, ds((j * QS + u) * TQ, TQ)]).then_inc(xq_loaded[u], 16)
                with sp.Fori(0, NT // 2) as j:
                    for u in range(2):
                        sp.wait_ge(unit_read, n * UNITS + j * (2 * SUB) + (SUB * u + SUB))
                        load_x(j * 2 + u, u)
                for cc in range(KC):
                    cu = cc % 2
                    for o, v_lines in enumerate((v_rows, v_cols)):
                        with sp.Fori(0, NG // 4) as g:
                            for v in range(4):
                                if cc == 0 and o == 0 and v == 0:
                                    sp.wait_ge(unit_read, n * UNITS + (UNITS + 4))
                                    for u in range(2):
                                        sp.wait_ge(v_stored[u], n * (8 * NT) + (160 + 16))
                                if cc == 0 and o == 0 and v == 2:
                                    for u in range(2):
                                        sp.wait_ge(v_stored[u], n * (8 * NT) + (8 * NT + 16))
                                sp.wait_ge(pair_ready, (g * 4 + v) + n * PAIR_READY + (READY_A + (2 * cc + o) * NG - 3))
                                sp.dma_start(vin[v][0:H, :, :], v_lines[n, cc, :, ds((g * 4 + v) * R, R), :]).then_inc(v_loaded[v], 16)
                            if o == 0 and 0 < cc < KC - 1:
                                cu = (cc + 1) % 2
                                half = HW * 4 // NG // 2
                                for h in range(2):
                                    sp.wait_ge(bank_ready, n * BANK_USES + (BANK_G + cc * NB + 2))
                                    sp.wait_ge(y_stored[cu], n * (Y_STORES * 16) + (Y_STORES * 8 + 16))
                                    sp.dma_start(qk[:, cu, ds(g * (2 * half) + h * half, half)],
                                                 x_px[n, :, cc + 1, ds(g * (2 * half) + h * half, half)]).then_inc(acc_loaded[cu], 16)
            sp.wait_ge(gram_added, N * KC + 1)
            sp.dma_start(gram_dram[:, :].rearrange("(k p) c -> p k c", p=P), gram_sb[:, :, :]).then_inc(gram_out, 16)
            sp.wait_ge(gram_out, 16)
            for u in range(2):
                sp.wait_ge(y_stored[u], N * Y_STORES * 16 + 16)
            g_rows = gram_dram[:, :].rearrange("(k b i) c -> b k i c", k=KC, b=BPC)
            for b in range(BPC):
                sp.dma_start(g_cov[b:GROUPS:BPC, :, :], g_rows[b, :, :, b * GS:(b + 1) * GS]).then_inc(gram_in, 16)
                sp.dma_start(g_low[b:GROUPS:BPC, :, :], g_rows[b, :, :, P + b * GS:P + (b + 1) * GS]).then_inc(gram_in, 16)
                sp.dma_start(g_sum[b:GROUPS:BPC, :].unsqueeze(2), g_rows[b, :, :, 2 * P:2 * P + 1], allow_slow_non_contiguous=True).then_inc(gram_in, 16)
            sp.wait_ge(fact_made, 1)
            sp.dma_start(wmat_dram[:, :, :], g_wt).then_inc(fact_out, 16)
            sp.dma_start(wbias_dram[:, :], g_bias).then_inc(fact_out, 16)
            sp.wait_ge(fact_out, 32)
            sp.wait_ge(wmat_zero, 1)
            for b in range(BPC):
                sp.dma_start(wmat[b * GS:(b + 1) * GS, :, b * GS:(b + 1) * GS],
                             wmat_dram[:, :, :].rearrange("(k b) j i -> b j k i", b=BPC)[b]).then_inc(fact_in, 16)
            sp.dma_start(wbias, wbias_dram[:, :].rearrange("(k b) i -> (b i) k", b=BPC), allow_slow_non_contiguous=True).then_inc(fact_in, 16)
            with sp.Fori(0, N) as n:
                for cc in range(KC):
                    for f in range(FN):
                        u = f % 2
                        sp.wait_ge(fin_ready[1], (n * (KC * FN) + (cc * FN + f + 1)) * HFB)
                        sp.dma_start(fy[:, u, :], y_dram[n, cc, :, f * FT:(f + 1) * FT]).then_inc(fy_loaded[u], 16)
            for u in range(2):
                sp.wait_ge(out_stored[u], 16 * N * KC * FN // 2 + 16)

        @block.gpsimd
        def _(pool):
            pool.memset(ident[:, :], 1.0).then_inc(consts_made, 1)
            pool.memset(gram_sb[:, :, :], 0.0).then_inc(consts_made, 1)
            pool.memset(ones_sq, 1.0).then_inc(consts_made, 1)
            pool.memset(ones_row[:, :], 1.0).then_inc(consts_made, 1)
            pool.memset(off_diag[:, :], 1.0).then_inc(consts_made, 1)
            pool.wait_ge(consts_made, 5)
            pool.affine_select(out=ident[:, :], in_=ident[:, :], compare_op=ALU.is_equal, fill=0.0, base=0,
                               pattern=[[-1, P]], channel_multiplier=1).then_inc(consts_made, 1)
            pool.affine_select(out=off_diag[:, :], in_=off_diag[:, :], compare_op=ALU.not_equal, fill=0.0, base=0,
                               pattern=[[-1, H]], channel_multiplier=1).then_inc(consts_made, 1)
            pool.wait_ge(consts_made, 7)
            with pool.Fori(0, N) as n:
                def low_part(t, u, q):
                    pool.wait_ge(xs_hi, n * UNITS + t * SUB + (q + 1))
                    pool.tensor_tensor(xs[:, q, 1, :, :], xt[:, u, :, q::SUB], xs[:, q, 0, :, :].bitcast(F32),
                                       ALU.subtract).then_inc(xs_lo, 1)

                def stage(i, v):
                    pool.wait_ge(factors, n * 2 + 2)
                    pool.wait_ge(bank_ready, n * BANK_USES + i * TPT + (v + 1))
                    l = i * (TPT * RT) + v * RT
                    pool.tensor_tensor(pstage[:, v, :, :], att_lines[:, ds(l, RT), :],
                                       factor[:, ds(l, RT)].unsqueeze(2).broadcast_to([H, RT, H]),
                                       ALU.mult).then_inc(staged, 1)

                for q in range(SUB):
                    low_part(0, 0, q)
                with pool.Fori(0, NG) as g:
                    pool.wait_ge(exp_done, n * 2 * NG + g + (NG + 1))
                    cols = att4[:, 1, ds(g * R, R), :]
                    pool.tensor_tensor(cols, cols, off_diag[:, :].unsqueeze(1).broadcast_to([H, R, H]), ALU.mult).then_inc(masked, 1)
                with pool.Fori(0, D_TURN // 2) as j:
                    for u in (1, 0):
                        for q in range(SUB):
                            low_part(j * 2 + (2 - u), u, q)
                with pool.Fori(0, (NT - D_TURN) // 2 - 1) as j:
                    for u in range(2):
                        for v in range(TPT):
                            stage(j * 2 + u, v)
                        for q in range(SUB):
                            low_part(j * 2 + (D_TURN + u + 1), 1 - u, q)
                for v in range(TPT):
                    stage(NT - 2 - D_TURN, v)
                for q in range(SUB):
                    low_part(NT - 1, 1, q)
                for v in range(TPT):
                    stage(NT - 1 - D_TURN, v)

        @block.scalar
        def _(act):
            act.sem_inc(qk_free, 2)
            for u in range(2):
                act.sem_inc(v_stored[u], 16)
                act.sem_inc(y_stored[u], 16)
                act.sem_inc(out_stored[u], 16)
            act.sem_inc(fin_free[0], 2)
            act.wait_ge(weights_scaled, 1)
            nc.scalar.copy(wv_hi[:, :, :], wv_gam).then_inc(weights_hi, 1)
            nc.scalar.activation(wv_abs, wv_gam, ACT.Abs).then_inc(weights_abs, 1)
            with act.Fori(0, N) as n:
                def high_part(t, u, q, load):
                    act.wait_ge(x_loaded[u], n * (NT * 8) + load * 16)
                    act.wait_ge(unit_read, n * UNITS + t * SUB + (q + 3))
                    nc.scalar.copy(xs[:, q, 0, :, :], xt[:, u, :, q::SUB]).then_inc(xs_hi, 1)

                def split_next(t, u):
                    for q in range(SUB):
                        high_part(t + 1, 1 - u, q, load_of(t + 1, 1 - u))

                def load_of(t, u):
                    return t // 2 + 1

                def values_high(t, u, store):
                    act.wait_ge(unit_read, n * UNITS + t * SUB + (SUB + 4))
                    act.wait_ge(v_stored[u], n * (8 * NT) + store * 16 + 16)
                    nc.scalar.activation(vout[:, u, :, :, 0, :].rearrange("p k s c -> p s k c"),
                                         pair[:, u, :, :].rearrange("p s (k c) -> p s k c", c=P),
                                         ACT.Identity, scale=v_up).then_inc(v_high, 1)

                def store_v(t, u):
                    act.wait_ge(pair_free, n * PAIR_USES + t + (PAIR_V + 3))
                    act.dma_start(v_tile[n, ds(t * P, P), :, :],
                                  vout[:, u, :, :, :, :].rearrange("p k s h c -> p k (s h c)")).then_inc(v_stored[u], 16)

                def turned_high(i, v):
                    act.wait_ge(bank_ready, n * BANK_USES + i * TPT + (v + 3))
                    nc.scalar.activation(att_parts[:, ds(i * (TPT * RT) + v * RT, RT), 0, :],
                                         bank[0:H, v, 0:RT * H].rearrange("p (r i) -> p r i", i=H),
                                         ACT.Copy, scale=ATT_UP).then_inc(bank_high, 1)

                def load_piece(t, cc):
                    act.dma_start(qk_flat[:, ds(t * PIECE, PIECE)],
                                  x_px[n, :, cc, ds(t * PIECE - cc * HW, PIECE)]).then_inc(acc_loaded[cc], 16)

                def bias_piece(i, cc):
                    act.wait_ge(acc_loaded[cc], n * (HALF_LOADS * 16) + HW // PIECE * 16)
                    part = qk_flat[:, ds(i * PIECE, PIECE)]
                    nc.scalar.activation(part, part, ACT.Identity, bias=out_bias[:, cc:cc + 1]).then_inc(biased, 1)

                act.wait_ge(y_stored[0], n * (Y_STORES * 16) + 16)
                act.wait_ge(y_stored[1], n * (Y_STORES * 16) + 16)
                with act.Fori(0, NQ // 2) as j:
                    for u in range(2):
                        t = j * 2 + u
                        act.wait_ge(qk_ready, n * NQ + t + 1)
                        nc.scalar.activation(qk[0:D, 0, ds(t * TQ, TQ)], bank[0:D, u, :], ACT.Identity, bias=cst[0:D, 0:1])
                        nc.scalar.activation(qk[0:D, 1, ds(t * TQ, TQ)], bank[D:2 * D, u, :], ACT.Identity,
                                             bias=cst[D:2 * D, 0:1]).then_inc(qk_free, 1)
                for q in range(SUB):
                    high_part(0, 0, q, 1)
                with act.Fori(0, 2 * NG) as g:
                    act.wait_ge(pair_free, n * PAIR_USES + g + 3)
                    flat = att[0:H, :, :].rearrange("p o i -> p (o i)")[:, ds(g * R * H, R * H)]
                    nc.scalar.activation(flat, flat, ACT.Exp).then_inc(exp_done, 1)
                split_next(0, 0)
                values_high(0, 0, 0)
                load_piece(0, 0)
                with act.Fori(0, D_STAT // 2 - 1) as j:
                    for u in (1, 0):
                        t = j * 2 + (2 - u)
                        for q in range(SUB):
                            high_part(t + 1, 1 - u, q, j + 2)
                        values_high(t, u, j + (1 - u))
                        store_v(t - 1, 1 - u)
                        load_piece(t, 0)
                for t in range(D_STAT - 1, D_TURN):
                    if t == D_STAT:
                        act.wait_ge(shift_done, n * 2 + 2)
                        nc.scalar.activation(shifted, shifted, ACT.Exp).then_inc(shift_exp, 1)
                    split_next(t, t % 2)
                    values_high(t, t % 2, t // 2)
                    store_v(t - 1, 1 - t % 2)
                    load_piece(t, 0)
                for cc, (a, b) in enumerate(((0, (NT - D_TURN) // 4), ((NT - D_TURN) // 4, (NT - D_TURN) // 2 - 1))):
                    with act.Fori(a, b) as j:
                        for u in range(2):
                            t = j * 2 + (D_TURN + u)
                            for q in range(SUB):
                                high_part(t + 1, 1 - u, q, j + (D_TURN // 2 + 1 + u))
                            values_high(t, u, j + D_TURN // 2)
                            store_v(t - 1, 1 - u)
                            if cc == 0:
                                load_piece(t, 1)
                            for v in range(TPT):
                                turned_high(j * 2 + u, v)
                            bias_piece(j * 2 + u, cc)
                for t in range(NT - 2, NT):
                    if t + 1 < NT:
                        split_next(t, t % 2)
                    values_high(t, t % 2, t // 2)
                    store_v(t - 1, 1 - t % 2)
                    if t + 1 == NT:
                        store_v(t, t % 2)
                    for v in range(TPT):
                        turned_high(t - D_TURN, v)
                    bias_piece(t - D_TURN, 1)
                for cc in range(KC):
                    cu = cc % 2
                    if 0 < cc < KC - 1:
                        act.wait_ge(acc_loaded[1 - cu], n * (HALF_LOADS * 16) + (cc + 1) // 2 * (2 * NG // 4 * 16) + HW // PIECE * 16)
                        nc.scalar.activation(qk[:, 1 - cu, :], qk[:, 1 - cu, :], ACT.Identity,
                                             bias=out_bias[:, cc + 1:cc + 2]).then_inc(biased, 1)
                    with act.Fori(0, NB // 3) as j:
                        act.wait_ge(pair_free, n * PAIR_USES + (PAIR_A + 2 + (cc + 1) * 2 * NG))
                        act.dma_start(y_dram[n, cc, :, ds(j * Y_PIECE, Y_PIECE)],
                                      qk[:, cu, ds(j * Y_PIECE, Y_PIECE)]).then_inc(y_stored[cu], 16)
                        for u in range(3):
                            act.wait_ge(bank_ready, n * BANK_USES + j * 3 + (BANK_G + cc * NB + u + 3))
                            act.wait_ge(ytr_free, n * (KC * NB) + j * 3 + (cc * NB + u + 1))
                            nc.scalar.activation(ytr_slots[u][:, :, 0:P], turn_ps[u].rearrange("p (s c) -> p s c", c=P),
                                                 ACT.Copy, scale=y_up).then_inc(bank_high, 1)
            act.wait_ge(sq_ready, 1)
            nc.scalar.activation(g_rt, g_piv, ACT.Sqrt).then_inc(sq_done, 1)
            act.wait_ge(fact_in, 16 * (BPC + 1))
            with act.Fori(0, N) as n:
                for cc in range(KC):
                    for f in range(FN):
                        u = f % 2
                        act.wait_ge(out_stored[u], (n * (KC * FN // 2) + (cc * FN // 2 + f // 2 + 1)) * 16)
                        for b in range(HFB):
                            act.wait_ge(fin_ready[0], n * (KC * FN * HFB) + ((cc * FN + f) * HFB + b + 1))
                            nc.scalar.activation(fo[:, u, 2 * b * FB:(2 * b + 1) * FB], bank[:, (f * HFB + b) % 2, 0:FB],
                                                 ACT.Identity, bias=wbias[:, cc:cc + 1]).then_inc(fin_free[0], 1)
                        for e in range(2):
                            act.wait_ge(fin_free[e], n * (KC * FN * HFB) + ((cc * FN + f + 1) * HFB + 2))
                        act.dma_start(out_px[n, cc, :, f * FT:(f + 1) * FT],
                                      fo[:, u, :]).then_inc(out_stored[u], 16)

        @block.vector
        def _(dve):
            nc.vector.sem_inc(pair_free, 2)
            nc.vector.sem_inc(bank_free, 2)
            nc.vector.sem_inc(gram_added, 1)
            nc.vector.sem_inc(fin_free[1], 2)
            steps = [0]

            def link(ins):
                steps[0] += 1
                ins.then_inc(chain, 1)
                dve.wait_ge(chain, steps[0])

            dve.wait_ge(consts_loaded, 8 * 16)
            nc.vector.tensor_scalar(wv_gam, wv_raw, gam, None, ALU.mult).then_inc(weights_scaled, 1)
            nc.vector.memset(ytr[:, :, :, 2 * P:GC], 1.0)
            nc.vector.tensor_scalar(out_bias, out_bias, gam, None, ALU.mult)
            link(nc.vector.tensor_scalar(bv_rep, bv_rep, gam, None, ALU.mult))
            link(nc.vector.tensor_reduce(bv_top, bv_rep, AX.X, ALU.max, apply_absolute_value=True))
            dve.wait_ge(weights_hi, 1)
            nc.vector.tensor_tensor(wv_lo[:, :, :], wv_gam, wv_hi[:, :, :].bitcast(F32), ALU.subtract).then_inc(weights_lo, 1)
            dve.wait_ge(norm_ready, 1)
            link(nc.vector.tensor_reduce(w_norm, stat_ps[:, 0:C], AX.X, ALU.max))
            dve.wait_ge(consts_made, 7)
            with dve.Fori(0, N) as n:
                def values_low(t, u):
                    dve.wait_ge(v_high, n * NT + t + 1)
                    for q in range(SUB):
                        last = nc.vector.scalar_tensor_tensor(
                            vout[:, u, :, q, 1, :], pair[:, u, q, :].rearrange("p (k c) -> p k c", c=P), v_up,
                            vout[:, u, :, q, 0, :], ALU.mult, ALU.subtract)
                    last.then_inc(pair_free, 1)

                def turned_low(i, v):
                    dve.wait_ge(bank_high, n * BANK_USES + i * TPT + (v + 1))
                    l = i * (TPT * RT) + v * RT
                    nc.vector.scalar_tensor_tensor(
                        att_parts[:, ds(l, RT), 1, :], bank[0:H, v, 0:RT * H].rearrange("p (r i) -> p r i", i=H), ATT_UP,
                        att_parts[:, ds(l, RT), 0, :], ALU.mult, ALU.subtract).then_inc(bank_free, 1)

                def small(k, ins, base):
                    ins.then_inc(chain, 1)
                    dve.wait_ge(chain, n * (SMALL + BOUNDS) + (CHAIN0 + base + k))

                with dve.Fori(0, NQ // QS) as j:
                    for u in range(QS):
                        dve.wait_ge(xq_loaded[u], n * (NQ // QS * 16) + j * 16 + 16)
                        nc.vector.tensor_reduce(xmax[:, ds(j * QS + u, 1)], xq[:, u, :, :], AX.XY, ALU.max,
                                                apply_absolute_value=True).then_inc(x_seen, 1)
                dve.wait_ge(x_seen, n * NQ + NQ)
                nc.vector.tensor_reduce(x_col, xmax[:, :], AX.X, ALU.max).then_inc(bound_m, 1)
                dve.wait_ge(bound_t, n * 2 + 1)
                nc.vector.tensor_reduce(x_top[0:1, :], stat_ps[0:1, 0:P], AX.X, ALU.max).then_inc(bound_m, 1)
                dve.wait_ge(bound_t, n * 2 + 2)
                small(1, nc.vector.tensor_copy(x_top, stat_ps[:, P:P + 1]), 0)
                small(2, nc.vector.tensor_scalar(v_top, x_top, w_norm, 1e-20, ALU.mult, ALU.max), 0)
                small(3, nc.vector.tensor_scalar(y_top, x_top, v_top, bv_top, ALU.add, ALU.add), 0)
                small(4, nc.vector.reciprocal(v_up, v_top), 0)
                small(5, nc.vector.reciprocal(y_up, y_top), 0)
                small(6, nc.vector.tensor_scalar(v_up, v_up, HALF_TOP, None, ALU.mult), 0)
                small(7, nc.vector.tensor_scalar(y_up, y_up, HALF_TOP, None, ALU.mult), 0)
                small(8, nc.vector.tensor_scalar(y_down, y_top, 1.0 / HALF_TOP, None, ALU.mult), 0)
                small(9, nc.vector.tensor_scalar(v_down, v_top, 1.0 / (HALF_TOP * ATT_UP), None, ALU.mult), 0)
                nc.vector.tensor_tensor(y_down2, y_down, y_down, ALU.mult).then_inc(bounds_done, 1)
                for o in range(2):
                    mx = max_r if o == 0 else max_c
                    with dve.Fori(0, NG // 2) as g:
                        for u in range(2):
                            l = (g * 2 + u) * R
                            dve.wait_ge(pair_ready, n * PAIR_READY + g * 2 + (o * NG + u + 1))
                            nc.vector.tensor_reduce(mx[:, ds(l, R)].rearrange("p (b r) -> p b r", b=2), lines(u, H), AX.X, ALU.max).then_inc(group_max, 1)
                            dve.wait_ge(group_max, n * 2 * NG + g * 2 + (o * NG + u + 1))
                            for b in range(2):
                                last = nc.vector.tensor_tensor(
                                    att4[:, o, ds(l + b * 4, 4), :], lines(u, H)[:, b],
                                    mx[:, ds(l + b * 4, 4)].unsqueeze(2).broadcast_to([H, 4, H]), ALU.subtract)
                            last.then_inc(pair_free, 1)
                for o in range(2):
                    with dve.Fori(0, D_STAT // 4) as j:
                        for u in range(2):
                            for e in range(SUMS):
                                g = j * (2 * SUMS) + (u * SUMS + e)
                                if o == 0:
                                    dve.wait_ge(exp_done, n * 2 * NG + g + 1)
                                else:
                                    dve.wait_ge(masked, n * NG + g + 1)
                                nc.vector.tensor_reduce((sum_r, sum_c)[o][:, ds(g * R, R)], att4[:, o, ds(g * R, R), :],
                                                        AX.X, ALU.add).then_inc(sums_done, 1)
                            values_low(j * 2 + (o * D_STAT // 2 + u), u)

                dve.wait_ge(stat_t, n * 2 + 1)
                max_ct, sum_ct, fac_ps = (stat_ps[0:H, i * H:(i + 1) * H] for i in range(3))
                small(1, nc.vector.tensor_tensor(joint, max_r, max_ct, ALU.max), BOUNDS)
                nc.vector.tensor_tensor(shifted[:, 0, :], max_r, joint, ALU.subtract).then_inc(shift_done, 1)
                nc.vector.tensor_tensor(shifted[:, 1, :], max_ct, joint, ALU.subtract).then_inc(shift_done, 1)
                dve.wait_ge(shift_exp, n + 1)
                nc.vector.tensor_tensor(fac_r, sum_r, shifted[:, 0, :], ALU.mult).then_inc(chain, 1)
                small(3, nc.vector.tensor_tensor(fac_ct, sum_ct, shifted[:, 1, :], ALU.mult), BOUNDS)
                small(4, nc.vector.tensor_tensor(joint, fac_r, fac_ct, ALU.add), BOUNDS)
                small(5, nc.vector.reciprocal(joint, joint), BOUNDS)
                nc.vector.tensor_tensor(fac_ct, shifted[:, 1, :], joint, ALU.mult).then_inc(chain, 1)
                nc.vector.tensor_tensor(fac_r, shifted[:, 0, :], joint, ALU.mult).then_inc(factors, 1)
                for t in range(D_STAT, D_FAC):
                    values_low(t, t % 2)
                dve.wait_ge(stat_t, n * 2 + 2)
                nc.vector.tensor_copy(fac_c, fac_ps).then_inc(factors, 1)
                for t in range(D_FAC, D_TURN):
                    values_low(t, t % 2)
                with dve.Fori(0, (NT - D_TURN) // 2) as j:
                    for u in range(2):
                        values_low(j * 2 + (D_TURN + u), u)
                        for v in range(TPT):
                            turned_low(j * 2 + u, v)
                nc.vector.memset(ytr_slots[2][:, :, 2 * P:GC], 1.0)
                for cc in range(KC):
                    cu = cc % 2
                    ready = BIASED - KC + 2 if cc >= 2 else 0
                    ready += cc - 1 if cc >= 2 else (cc + 1) * (HW // PIECE)
                    for o in range(2):
                        with dve.Fori(0, NG // 3) as g:
                            if o == 0:
                                dve.wait_ge(biased, n * BIASED + ready)
                            else:
                                dve.wait_ge(pair_free, n * PAIR_USES + (PAIR_A + 2 + (2 * cc + 1) * NG))
                            for u in range(3):
                                dve.wait_ge(pair_ready, n * PAIR_READY + g * 3 + (READY_A + (2 * cc + o) * NG + u + 1))
                                l = (g * 3 + u) * R
                                if o == 0:
                                    dst = qk[:, cu, ds(l * W, R * W)].rearrange("p (b i) -> p b i", b=2)
                                    last = nc.vector.scalar_tensor_tensor(dst, agg_ps[u][:, :, 0:4 * W], v_down, dst, ALU.mult, ALU.add)
                                else:
                                    for b in range(2):
                                        dst = acc4[:, cu, :, ds(l + b * 4, 4)].rearrange("p y r -> p r y")
                                        last = nc.vector.scalar_tensor_tensor(dst, agg_lines(u)[:, b], v_down, dst, ALU.mult, ALU.add)
                                last.then_inc(pair_free, 1)
                    with dve.Fori(0, NB // 3) as j:
                        for u in range(3):
                            dve.wait_ge(bank_high, n * BANK_USES + j * 3 + (BANK_G + cc * NB + u + 1))
                            nc.vector.scalar_tensor_tensor(ytr_slots[u][:, :, P:2 * P], turn_ps[u].rearrange("p (s c) -> p s c", c=P),
                                                           y_up, ytr_slots[u][:, :, 0:P], ALU.mult, ALU.subtract).then_inc(bank_free, 1)
                    dve.wait_ge(ytr_free, n * (KC * NB) + ((cc + 1) * NB + 3))
                    nc.vector.scalar_tensor_tensor(gram_sb[:, cc, 2 * P:GC], gram_ps[:, 2 * P:GC], y_down,
                                                   gram_sb[:, cc, 2 * P:GC], ALU.mult, ALU.add)
                    nc.vector.scalar_tensor_tensor(gram_sb[:, cc, 0:2 * P], gram_ps[:, 0:2 * P], y_down2,
                                                   gram_sb[:, cc, 0:2 * P], ALU.mult, ALU.add).then_inc(gram_added, 1)
            steps[0] = CHAIN0 + N * (SMALL + BOUNDS)
            INV = 1.0 / (N * HW)
            dve.wait_ge(gram_in, 48 * BPC)
            link(nc.vector.tensor_tensor(g_cov, g_cov, g_low, ALU.add))
            link(nc.vector.tensor_tensor(g_cov, g_cov, g_low.rearrange("p i j -> p j i"), ALU.add))
            link(nc.vector.tensor_scalar(g_mean, g_sum, INV, None, ALU.mult))
            link(nc.vector.tensor_tensor(g_tmp, g_mean.unsqueeze(2).broadcast_to([GROUPS, GS, GS]),
                                         g_mean.unsqueeze(1).broadcast_to([GROUPS, GS, GS]), ALU.mult))
            link(nc.vector.tensor_scalar(g_cov, g_cov, INV, None, ALU.mult))
            link(nc.vector.tensor_tensor(g_cov, g_cov, g_tmp, ALU.subtract))
            link(nc.vector.memset(g_eye, 0.0))
            link(nc.vector.memset(qk[0:GROUPS, 0, 3072:3072 + GS * GS:GS + 1], 1.0))
            link(nc.vector.tensor_scalar(g_aug[:, :, 0:GS], g_cov, 1.0 - EPS, None, ALU.mult))
            link(nc.vector.tensor_scalar(g_tmp, g_eye, EPS, None, ALU.mult))
            link(nc.vector.tensor_tensor(g_aug[:, :, 0:GS], g_aug[:, :, 0:GS], g_tmp, ALU.add))
            link(nc.vector.tensor_copy(g_aug[:, :, GS:2 * GS], g_eye))
            for k in range(GS - 1):
                m = GS - 1 - k
                link(nc.vector.reciprocal(g_rec, g_aug[:, k, k:k + 1]))
                link(nc.vector.tensor_scalar(g_fac[:, 0:m].unsqueeze(2), g_aug[:, k + 1:GS, k:k + 1], g_rec, None, ALU.mult))
                link(nc.vector.tensor_tensor(g_tmp[:, 0:m, :], g_fac[:, 0:m].unsqueeze(2).broadcast_to([GROUPS, m, GS]),
                                             g_aug[:, k, k + 1:k + 1 + GS].unsqueeze(1).broadcast_to([GROUPS, m, GS]), ALU.mult))
                link(nc.vector.tensor_tensor(g_aug[:, k + 1:GS, k + 1:k + 1 + GS], g_aug[:, k + 1:GS, k + 1:k + 1 + GS],
                                             g_tmp[:, 0:m, :], ALU.subtract))
            nc.vector.tensor_copy(g_piv, qk[0:GROUPS, 0, 1024:1024 + 2 * GS * GS:2 * GS + 1]).then_inc(sq_ready, 1)
            dve.wait_ge(sq_done, 1)
            link(nc.vector.reciprocal(g_piv, g_rt))
            link(nc.vector.tensor_tensor(g_wt, g_aug[:, :, GS:2 * GS].rearrange("p i j -> p j i"),
                                         g_piv.unsqueeze(1).broadcast_to([GROUPS, GS, GS]), ALU.mult))
            link(nc.vector.tensor_tensor(g_tmp, g_wt.rearrange("p j i -> p i j"),
                                         g_mean.unsqueeze(1).broadcast_to([GROUPS, GS, GS]), ALU.mult))
            nc.vector.tensor_reduce(g_bias, g_tmp, AX.X, ALU.add, negate=True).then_inc(fact_made, 1)
            nc.vector.memset(wmat, 0.0).then_inc(wmat_zero, 1)
            dve.wait_ge(fact_in, 16 * (BPC + 1))
            with dve.Fori(0, N) as n:
                for cc in range(KC):
                    for f in range(FN):
                        u = f % 2
                        dve.wait_ge(out_stored[u], (n * (KC * FN // 2) + (cc * FN // 2 + f // 2 + 1)) * 16)
                        for b in range(HFB):
                            dve.wait_ge(fin_ready[1], n * (KC * FN * HFB) + ((cc * FN + f + 2) * HFB + b + 1))
                            nc.vector.tensor_scalar(fo[:, u, (2 * b + 1) * FB:(2 * b + 2) * FB],
                                                    pair[:, (f * HFB + b) % 2, 0, 0:FB],
                                                    wbias[:, cc:cc + 1], None, ALU.add).then_inc(fin_free[1], 1)

        @block.tensor
        def _(pe):
            pe.sem_inc(unit_read, 4)
            pe.sem_inc(ytr_free, 3)
            pe.wait_ge(consts_loaded, 8 * 16)
            pe.sem_inc(bank_ready, 2)
            pe.wait_ge(weights_lo, 1)
            pe.wait_ge(consts_made, 7)

            pe.wait_ge(weights_abs, 1)
            for k in range(KC):
                last = nc.tensor.matmul(stat_ps[:, 0:C], ones_sq, wv_abs[:, k, :], start=k == 0, stop=k == KC - 1)
            last.then_inc(norm_ready, 1)

            with pe.Fori(0, N) as n:
                def project_v(t, u):
                    pe.wait_ge(pair_free, n * PAIR_USES + t + (PAIR_V + 1))
                    for q in range(SUB):
                        pe.wait_ge(xs_lo, n * UNITS + t * SUB + (q + 1))
                        terms = [(xs[:, q, a, k, :], w[:, k, :]) for k in range(KC)
                                 for a, w in ((1, wv_hi), (0, wv_lo), (0, wv_hi))]
                        for i, (lhs, rhs) in enumerate(terms):
                            last = nc.tensor.matmul(pair[:, u, q, :], lhs, rhs, start=i == 0, stop=i == len(terms) - 1)
                        last.then_inc(unit_read, 1)

                with pe.Fori(0, NQ // QS) as j:
                    for u in range(QS):
                        pe.wait_ge(xq_loaded[u], n * (NQ // QS * 16) + j * 16 + 16)
                        pe.wait_ge(bank_free, n * BANK_USES + 2)
                        pe.wait_ge(qk_free, n * NQ + j * QS + (u + 1))
                        for k in range(KC):
                            last = nc.tensor.matmul(bank[:, u % 2, :], wqk[:, k, :], xq[:, u, k, :], start=k == 0, stop=k == KC - 1)
                        last.then_inc(qk_ready, 1)
                pe.wait_ge(bound_m, n * 2 + 1)
                nc.tensor.transpose(stat_ps[0:1, 0:P], x_col, ident[:, :]).then_inc(bound_t, 1)
                pe.wait_ge(bound_m, n * 2 + 2)
                nc.tensor.matmul(stat_ps[:, P:P + 1], ones_row[:, :], x_top[0:1, :], start=True, stop=True).then_inc(bound_t, 1)
                for e in range(2 * NG):
                    o, g = divmod(e, NG)
                    if e == 0:
                        pe.wait_ge(qk_free, n * NQ + (NQ + 2))
                    pe.wait_ge(pair_free, n * PAIR_USES + (e + 1))
                    for r in range(R):
                        last = nc.tensor.matmul(lines(e % 2, H)[:, r // 4, r % 4, :], q_ori[o][:, g * R + r, :],
                                                k_ori[o][:, g * R + r, :], start=True, stop=True)
                    last.then_inc(pair_ready, 1)

                with pe.Fori(0, D_STAT // 2) as j:
                    for u in range(2):
                        project_v(j * 2 + u, u)
                pe.wait_ge(sums_done, n * 2 * NG + 2 * NG)
                nc.tensor.transpose(stat_ps[0:H, 0:H], max_c, ident[0:H, 0:H])
                nc.tensor.transpose(stat_ps[0:H, H:2 * H], sum_c, ident[0:H, 0:H]).then_inc(stat_t, 1)
                for t in range(D_STAT, D_FAC):
                    project_v(t, t % 2)
                pe.wait_ge(chain, n * (SMALL + BOUNDS) + (CHAIN0 + BOUNDS + 6))
                nc.tensor.transpose(stat_ps[0:H, 2 * H:3 * H], fac_ct, ident[0:H, 0:H]).then_inc(stat_t, 1)
                for t in range(D_FAC, D_TURN):
                    project_v(t, t % 2)
                with pe.Fori(0, (NT - D_TURN) // 2) as j:
                    for u in range(2):
                        project_v(j * 2 + (D_TURN + u), u)
                        for v in range(TPT):
                            pe.wait_ge(staged, n * NTR + j * (2 * TPT) + (u * TPT + v + 1))
                            pe.wait_ge(bank_free, n * BANK_USES + j * (2 * TPT) + (u * TPT + v + 1))
                            for r in range(RT):
                                last = nc.tensor.transpose(bank[0:H, v, r * H:(r + 1) * H], pstage[:, v, r, :], ident[0:H, 0:H])
                            last.then_inc(bank_ready, 1)

                with pe.Fori(0, KC // 2) as cp:
                    for cu in range(2):
                        for a in range(2 * NG):
                            o, g = divmod(a, NG)
                            v = g % 4
                            if a == 0:
                                pe.wait_ge(bank_free, n * BANK_USES + (BANK_G + 2))
                            pe.wait_ge(v_loaded[v], n * (KC * NG // 2 * 16) + cp * (NG * 16) + (cu * (NG // 2) + a // 4 + 1) * 16)
                            if a < 3:
                                pe.wait_ge(pair_free, n * PAIR_USES + cp * (4 * NG) + (PAIR_A + cu * 2 * NG + 2))
                                pe.wait_ge(bank_free, n * BANK_USES + cp * (2 * NB) + (BANK_G + cu * NB + 2))
                            else:
                                pe.wait_ge(pair_free, n * PAIR_USES + cp * (4 * NG) + (PAIR_A + cu * 2 * NG + a))
                            for r in range(R):
                                for i, (vh, ah) in enumerate(((1, 0), (0, 1), (0, 0))):
                                    last = nc.tensor.matmul(agg_lines(a % 3)[:, r // 4, r % 4, :],
                                                            vin[v][0:H, r, vh * P:(vh + 1) * P],
                                                            att_parts[:, a * R + r, ah, :], start=i == 0, stop=i == 2)
                            last.then_inc(pair_ready, 1)

                        def turn(b):
                            if b == 0:
                                pe.wait_ge(pair_free, n * PAIR_USES + cp * (4 * NG) + (PAIR_A + 2 + (cu + 1) * 2 * NG))
                            pe.wait_ge(bank_free, n * BANK_USES + cp * (2 * NB) + (BANK_G + cu * NB + max(b, 2)))
                            for s in range(SB):
                                last = nc.tensor.transpose(turn_ps[b % 3][:, s * P:(s + 1) * P],
                                                           qk[:, cu, (b * SB + s) * P:(b * SB + s + 1) * P], ident[:, :])
                            last.then_inc(bank_ready, 1)

                        def products(b):
                            if b == 0:
                                pe.wait_ge(gram_added, n * KC + cp * 2 + (cu + 1))
                            pe.wait_ge(bank_free, n * BANK_USES + cp * (2 * NB) + (BANK_G + cu * NB + b + 3))
                            for s in range(SB):
                                nc.tensor.matmul(gram_ps[:, 0:GC], ytr_slots[b % 3][:, s, 0:P], ytr_slots[b % 3][:, s, :],
                                                 start=b == 0 and s == 0, stop=False, skip_group_check=True)
                                last = nc.tensor.matmul(gram_ps[:, 2 * P:GC], ytr_slots[b % 3][:, s, P:2 * P], ytr_slots[b % 3][:, s, 2 * P:GC],
                                                        start=False, stop=b == NB - 1 and s == SB - 1, skip_group_check=True)
                            last.then_inc(ytr_free, 1)

                        turn(0)
                        turn(1)
                        for b in range(NB):
                            if b + 2 < NB:
                                turn(b + 2)
                            products(b)
            pe.sem_inc(fin_ready[1], 2 * HFB)
            pe.wait_ge(fact_in, 16 * (BPC + 1))
            with pe.Fori(0, N) as n:
                for cc in range(KC):
                    for f in range(FN):
                        u = f % 2
                        pe.wait_ge(fy_loaded[u], (n * (KC * FN // 2) + (cc * FN // 2 + f // 2 + 1)) * 16)
                        for b in range(HFB):
                            for e, dst in enumerate((bank[:, (f * HFB + b) % 2, 0:FB], pair[:, (f * HFB + b) % 2, 0, 0:FB])):
                                pe.wait_ge(fin_free[e], n * (KC * FN * HFB) + ((cc * FN + f) * HFB + b + 1))
                                nc.tensor.matmul(dst, wmat[:, cc, :], fy[:, u, (2 * b + e) * FB:(2 * b + e + 1) * FB],
                                                 start=True, stop=True).then_inc(fin_ready[e], 1)


def kernel(**inputs):
    import concourse.bacc as bacc
    from concourse.bass_utils import run_bass_kernel_spmd

    nc = bacc.Bacc("TRN2", target_bir_lowering=False, num_devices=1)
    arrays = {
        "x": np.ascontiguousarray(inputs["x"]),
        "wq_t": np.ascontiguousarray(np.asarray(inputs["L0_conv_wq"]).T),
        "bq": np.ascontiguousarray(inputs["L0_conv_bq"]),
        "wk_t": np.ascontiguousarray(np.asarray(inputs["L0_conv_wk"]).T),
        "bk": np.ascontiguousarray(inputs["L0_conv_bk"]),
        "wv_t": np.ascontiguousarray(np.asarray(inputs["L0_conv_wv"]).T),
        "bv": np.ascontiguousarray(inputs["L0_conv_bv"]),
        "gamma": np.asarray(inputs["L0_conv_gamma"]).reshape(1),
    }
    args = [nc.dram_tensor(name, a.shape, mybir.dt.from_np(a.dtype), kind="ExternalInput").ap()
            for name, a in arrays.items()]
    out = nc.dram_tensor("out", arrays["x"].shape, mybir.dt.float32, kind="ExternalOutput")
    criss_cross_whitening_kernel(nc, *args, out.ap())
    result = run_bass_kernel_spmd(nc, [arrays], core_ids=[0])
    return result.results[0]["out"]
```

```python
from contextlib import ExitStack

import numpy as np

import concourse.bass as bass
from concourse import mybir


def criss_cross_whitening_kernel(nc, x, wq_t, bq, wk_t, bk, wv_t, bv, gamma, out):
    F32 = mybir.dt.float32
    F16 = mybir.dt.float16
    F32R = mybir.dt.float32r
    ALU = mybir.AluOpType
    ACT = mybir.ActivationFunctionType
    AX = mybir.AxisListType
    ds = bass.ds

    N, C, H, W = x.shape
    P = 128
    HW = H * W
    D = wq_t.shape[1]
    KC = C // P
    TP = 256
    NT = HW // TP
    SUB = TP // P
    TQ = 384
    NQ = HW // TQ
    QS = 6
    R = 8
    NG = H // R
    LS = 128
    RT = 4
    NTR = 2 * H // RT
    TB = 512
    NB = HW // TB
    SB = TB // P
    GS, EPS = 16, 0.001
    GROUPS = C // GS
    BPC = P // GS
    GC = 2 * P + 2
    HALF_TOP = 2.0 ** 15
    ATT_UP = 2.0 ** 14
    QP = 6
    PX = HW // QP
    assert NG % QP == 0 and NG // 4 == 3 and NG % 6 == 0 and NQ % QS == 0 and NB % 3 == 0 and NG % 3 == 0
    assert H == W and NT % 6 == 0 and NB % 2 == 0 and NG % 4 == 0 and H % R == 0 and KC % 2 == 0

    PAIR_V = 2 * NG
    PAIR_A = PAIR_V + NT
    PAIR_USES = PAIR_A + KC * 2 * NG
    READY_A = 2 * NG
    PAIR_READY = READY_A + KC * 2 * NG
    BANK_G = NTR
    BANK_USES = BANK_G + KC * NB
    UNITS = SUB * NT
    D_STAT = 8
    D_FAC = 10
    D_TURN = 12
    TPT = NTR // (NT - D_TURN)
    GE = 6
    V_FIRST = 2
    SUMS = 2 * NG // (D_STAT - V_FIRST)
    Y_PIECE = 3 * TB
    YP = HW // Y_PIECE
    RES = [range(0, YP - 2), range(YP - 2, YP - 1), range(YP - 1, YP)]
    BIASED = NT - V_FIRST + KC - 2
    SMALL = 6
    CHAIN0 = 5
    BOUNDS = 14
    assert TPT == 2 and SUMS * (D_STAT - V_FIRST) == 2 * NG and NG % SUMS == 0

    x_px = x.rearrange("n (k p) h w -> n p k (h w)", p=P)
    out_px = out.rearrange("n (k p) h w -> n k p (h w)", p=P)
    v_dram = nc.dram_tensor("v_dram", [N, KC, HW, 2, P], F16)
    y_dram = nc.dram_tensor("y_dram", [N, KC, P, HW], F32)
    v_rows = v_dram[:, :, :, :, :].rearrange("n k (y x) h c -> n k x y (h c)", x=W)
    v_cols = v_dram[:, :, :, :, :].rearrange("n k (y x) h c -> n k y x (h c)", x=W)
    v_tile = v_dram[:, :, :, :, :].rearrange("n k (q s) h c -> n q k (s h c)", s=SUB)
    gram_dram = nc.dram_tensor("gram_dram", [C, GC], F32)
    wmat_dram = nc.dram_tensor("wmat_dram", [GROUPS, GS, GS], F32)
    wbias_dram = nc.dram_tensor("wbias_dram", [GROUPS, GS], F32)

    ctx = ExitStack()
    with ctx:
        def sb(name, shape):
            return ctx.enter_context(nc.sbuf_tensor(name, shape, F32))

        def sem(name):
            return ctx.enter_context(nc.semaphore(name))

        qk = sb("qk", [P, 2, HW])
        att = sb("att", [P, 2, HW])
        wqk = sb("wqk", [P, KC, 2 * D])
        wv_hi = ctx.enter_context(nc.sbuf_tensor("wv_hi", [P, KC, C], F32R))
        wv_lo = ctx.enter_context(nc.sbuf_tensor("wv_lo", [P, KC, C], F32R))
        xt = sb("xt", [P, 2, KC, TP])
        xs = ctx.enter_context(nc.sbuf_tensor("xs", [P, 2, 2, KC, P], F32R))
        vbuf = ctx.enter_context(nc.sbuf_tensor("vbuf", [P, 2 * R * 2 * P], F16))
        ytr = ctx.enter_context(nc.sbuf_tensor("ytr", [P, 2, SB, GC], F16))
        pbuf = sb("pbuf", [P, 2 * RT * H])
        pstage = pbuf[0:H, :].rearrange("p (v r i) -> p v r i", v=2, r=RT)
        ytr_slots = [ytr[:, 0, :, :], ytr[:, 1, :, :],
                     pbuf[:, :].bitcast(F16)[:, 0:SB * GC].rearrange("p (s c) -> p s c", s=SB)]
        xmax = sb("xmax", [P, NQ])
        ones_row = sb("ones_row", [1, P])
        ident = sb("ident", [P, P])
        off_diag = sb("off_diag", [H, H])
        stat = sb("stat", [P, 10, H])
        gram_sb = sb("gram_sb", [P, KC, GC])
        cst = sb("cst", [P, 26])

        vout = vbuf[:, :].rearrange("p (u k s h c) -> p u k s h c", u=2, k=KC, s=SUB, h=2)
        xt_halves = xt[:, :, :, :].bitcast(F16).rearrange("p u k t -> p u (k t)")
        xs_halves = xs[:, :, :, :, :].bitcast(F16).rearrange("p u h k c -> p u (h k c)")
        vin = [place[:, u, :].rearrange("p (r c) -> p r c", r=R) for place in (xt_halves, xs_halves) for u in range(2)]
        xq = att[:, 0, 0:QS * KC * TQ].rearrange("p (u k t) -> p u k t", u=QS, k=KC)
        wv_raw = qk[:, 0, 0:KC * C].rearrange("p (k c) -> p k c", k=KC)
        wv_gam = qk[:, 1, 0:KC * C].rearrange("p (k c) -> p k c", k=KC)
        wv_abs = qk[:, 0, KC * C:2 * KC * C].rearrange("p (k c) -> p k c", k=KC)
        ones_sq = qk[:, 1, KC * C:KC * C + P]
        bv_rep = qk[:, 1, KC * C + P:KC * C + P + C]
        qk_raw = att[:, 1, :]
        qk_hi, qk_lo, k_hi, k_lo = (qk[:, :, :].rearrange("p u i -> p (u i)").bitcast(F16)[:, i * HW:(i + 1) * HW] for i in range(4))
        wqk_abs = qk[:, 1, KC * C + P + C:KC * C + P + C + KC * 2 * D].rearrange("p (k d) -> p k d", k=KC)
        bqk_abs = qk[:, 1, KC * C + P + C + KC * 2 * D:KC * C + P + C + KC * 2 * D + 1]

        def qk_line(part, o, l):
            grid = part[0:D, :].rearrange("p (y x) -> p y x", x=W)
            return grid[:, l, :] if o == 0 else grid[:, :, l]

        att_lines = att[0:H, :, :].rearrange("p o (l i) -> p (o l) i", i=H)
        att_parts = att[0:H, :, :].bitcast(F16).rearrange("p o (l h i) -> p (o l) h i", h=2, i=H)
        att4 = att[0:H, :, :].rearrange("p o (l i) -> p o l i", i=H)
        acc4 = qk[:, :, :].rearrange("p u (y x) -> p u y x", x=W)
        max_r, sum_r, max_c, sum_c, joint, fac_ct, fac_r, fac_c = (stat[0:H, i, :] for i in range(8))
        factor = stat[0:H, 6:8, :].rearrange("p o l -> p (o l)")
        shifted = stat[0:H, 8:10, :]
        bias_qk, gam = cst[:, 0:1], cst[:, 1:2]
        w_norm, bv_top = cst[:, 2:3], cst[:, 3:4]
        out_bias = cst[:, 8:12]
        v_up, v_down, y_up, y_down, y_down2, x_top, v_top, y_top, x_col = (cst[:, i:i + 1] for i in range(12, 21))
        qk_up, e_down, qk_top = (cst[:, i:i + 1] for i in range(21, 24))
        wqk_norm, bqk_sum = cst[:, 24:25], cst[:, 25:26]

        pair = ctx.enter_context(nc.psum_tensor("pair", [P, 2, 2, 512], F32))
        bank = ctx.enter_context(nc.psum_tensor("bank", [P, 2, 512], F32))
        gram_ps = ctx.enter_context(nc.psum_tensor("gram_ps", [P, 512], F32))
        stat_ps = ctx.enter_context(nc.psum_tensor("stat_ps", [P, 512], F32))

        pair_ps = [pair[:, 0, :, :], pair[:, 1, :, :], bank[:, :, :]]
        turn_ps = [bank[:, 0, :], bank[:, 1, :], stat_ps[:, :]]

        def pair_lines(v):
            return pair_ps[v].rearrange("p b (r i) -> p (b r) i", i=LS)[:, :, 0:H]

        consts_loaded = sem("consts_loaded")
        consts_made = sem("consts_made")
        weights_scaled = sem("weights_scaled")
        weights_hi = sem("weights_hi")
        weights_lo = sem("weights_lo")
        x_loaded = [sem(f"x_loaded{u}") for u in range(2)]
        xq_loaded = [sem(f"xq_loaded{u}") for u in range(QS)]
        xs_hi = sem("xs_hi")
        xs_lo = sem("xs_lo")
        unit_read = sem("unit_read")
        pair_ready = sem("pair_ready")
        pair_free = sem("pair_free")
        qk_ready = sem("qk_ready")
        qk_free = sem("qk_free")
        qk_high = sem("qk_high")
        qk_low = sem("qk_low")
        keys_moved = [sem(f"keys_moved{i}") for i in range(QP)]
        edge_loaded = sem("edge_loaded")
        bank_ready = sem("bank_ready")
        bank_high = sem("bank_high")
        bank_free = sem("bank_free")
        v_high = sem("v_high")
        x_seen = sem("x_seen")
        norm_ready = sem("norm_ready")
        weights_abs = sem("weights_abs")
        bound_t = sem("bound_t")
        bound_m = sem("bound_m")
        bounds_done = sem("bounds_done")
        biased = sem("biased")
        v_stored = [sem(f"v_stored{u}") for u in range(2)]
        v_loaded = [sem(f"v_loaded{u}") for u in range(4)]
        group_max = sem("group_max")
        exp_done = sem("exp_done")
        masked = sem("masked")
        sums_done = sem("sums_done")
        stat_t = sem("stat_t")
        shift_done = sem("shift_done")
        shift_exp = sem("shift_exp")
        chain = sem("chain")
        factors = sem("factors")
        staged = sem("staged")
        acc_loaded = [sem(f"acc_loaded{u}") for u in range(2)]
        y_stored = [[sem(f"y_stored{u}_{p}") for p in range(YP)] for u in range(2)]
        ytr_free = sem("ytr_free")
        gram_added = sem("gram_added")
        gram_out = sem("gram_out")
        gram_in = sem("gram_in")
        fact_made = sem("fact_made")
        fact_out = sem("fact_out")
        fact_in = sem("fact_in")
        sq_ready = sem("sq_ready")
        sq_done = sem("sq_done")
        wmat_zero = sem("wmat_zero")
        fy_loaded = [sem(f"fy_loaded{u}") for u in range(2)]
        fin_ready = [sem("fin_ready_act"), sem("fin_ready_dve")]
        fin_free = [sem("fin_free_act"), sem("fin_free_dve")]
        out_stored = [sem(f"out_stored{u}") for u in range(2)]

        FT = 2304
        FN = HW // FT
        FB = 384
        HFB = FT // FB // 2
        fy = att[:, 0, 0:2 * FT].rearrange("p (u c) -> p u c", u=2)
        fo = att[:, 1, 0:2 * FT].rearrange("p (u c) -> p u c", u=2)
        wmat = vbuf[:, :].bitcast(F32)[:, 0:KC * P].rearrange("p (k c) -> p k c", k=KC)
        wbias = cst[:, 4:8]
        g_cov = qk[0:GROUPS, 0, 0:GS * GS].rearrange("p (i j) -> p i j", j=GS)
        g_sum = qk[0:GROUPS, 0, 256:256 + GS]
        g_mean = qk[0:GROUPS, 0, 272:272 + GS]
        g_tmp = qk[0:GROUPS, 0, 512:512 + GS * GS].rearrange("p (i j) -> p i j", j=GS)
        g_aug = qk[0:GROUPS, 0, 1024:1024 + 2 * GS * GS].rearrange("p (i j) -> p i j", j=2 * GS)
        g_fac = qk[0:GROUPS, 0, 2048:2048 + GS]
        g_piv = qk[0:GROUPS, 0, 2064:2064 + GS]
        g_rt = qk[0:GROUPS, 0, 2080:2080 + GS]
        g_bias = qk[0:GROUPS, 0, 2096:2096 + GS]
        g_rec = qk[0:GROUPS, 0, 2112:2113]
        g_low = qk[0:GROUPS, 0, 3584:3584 + GS * GS].rearrange("p (i j) -> p i j", j=GS)
        g_wt = qk[0:GROUPS, 0, 2560:2560 + GS * GS].rearrange("p (j i) -> p j i", i=GS)
        g_eye = qk[0:GROUPS, 0, 3072:3072 + GS * GS].rearrange("p (i j) -> p i j", j=GS)

        block = ctx.enter_context(nc.Block())

        @block.sync
        def _(sp):
            sp.dma_start(wqk[:, :, 0:D], wq_t.rearrange("(k p) d -> p k d", p=P)).then_inc(consts_loaded, 16)
            sp.dma_start(wqk[:, :, D:2 * D], wk_t.rearrange("(k p) d -> p k d", p=P)).then_inc(consts_loaded, 16)
            sp.dma_start(wv_raw, wv_t.rearrange("(k p) d -> p k d", p=P)).then_inc(consts_loaded, 16)
            sp.dma_start(cst[0:D, 0:1], bq.rearrange("(d a) -> d a", a=1)).then_inc(consts_loaded, 16)
            sp.dma_start(cst[D:2 * D, 0:1], bk.rearrange("(d a) -> d a", a=1)).then_inc(consts_loaded, 16)
            sp.dma_start(cst[:, 1:2], gamma.rearrange("(a b) -> a b", b=1).broadcast_to([P, 1])).then_inc(consts_loaded, 16)
            sp.dma_start(out_bias, bv.rearrange("(k p) -> p k", p=P), allow_slow_non_contiguous=True).then_inc(consts_loaded, 16)
            sp.dma_start(bv_rep, bv.rearrange("(a c) -> a c", a=1).broadcast_to([P, C])).then_inc(consts_loaded, 16)

            with sp.Fori(0, N) as n:
                def load_x(t, u):
                    sp.dma_start(xt[:, u, :, :], x_px[n, :, :, ds(t * TP, TP)]).then_inc(x_loaded[u], 16)

                for u in range(QS):
                    sp.wait_ge(pair_free, n * PAIR_USES + 2)
                    sp.dma_start(xq[:, u, :, :], x_px[n, :, :, u * TQ:(u + 1) * TQ]).then_inc(xq_loaded[u], 16)
                for a, b in ((1, 2), (2, NQ // QS)):
                    with sp.Fori(a, b) as j:
                        for u in range(QS):
                            sp.wait_ge(x_seen, n * NQ + j * QS + (u + 1 - QS))
                            sp.wait_ge(qk_ready, n * NQ + j * QS + (u + 1 - QS))
                            sp.dma_start(xq[:, u, :, :], x_px[n, :, :, ds((j * QS + u) * TQ, TQ)]).then_inc(xq_loaded[u], 16)
                    if a == 1:
                        for u in range(V_FIRST):
                            sp.wait_ge(unit_read, n * UNITS + (SUB * u + SUB))
                            load_x(u, u)
                with sp.Fori(V_FIRST // 2, NT // 2) as j:
                    for u in range(2):
                        sp.wait_ge(unit_read, n * UNITS + j * (2 * SUB) + (SUB * u + SUB))
                        sp.wait_ge(biased, (j * 2 + u) + n * BIASED + 1)
                        load_x(j * 2 + u, u)
                def load_v(cc, o, g, v):
                    if cc == 0 and o == 0:
                        for u in range(2):
                            sp.wait_ge(v_stored[u], n * (8 * NT) + (8 * NT + 16))
                    sp.wait_ge(pair_ready, (g * 4 + v) + n * PAIR_READY + (READY_A + (2 * cc + o) * NG - 3))
                    fetch_v(cc, o, g, v)

                def fetch_v(cc, o, g, v):
                    sp.dma_start(vin[v][0:H, :, :], (v_rows, v_cols)[o][n, cc, :, ds((g * 4 + v) * R, R), :]).then_inc(v_loaded[v], 16)

                def load_residual(cc, p):
                    sp.wait_ge(bank_ready, n * BANK_USES + (BANK_G + (cc - 2) * NB + p * 3 + 5))
                    sp.wait_ge(y_stored[cc % 2][p], n * (KC // 2 * 16) + 32)
                    sp.dma_start(qk[:, cc % 2, p * Y_PIECE:(p + 1) * Y_PIECE],
                                 x_px[n, :, cc, p * Y_PIECE:(p + 1) * Y_PIECE]).then_inc(acc_loaded[cc % 2], 16)

                for cc in range(KC):
                    for o in range(2):
                        if cc == 0 and o == 0:
                            sp.wait_ge(xs_lo, n * UNITS + UNITS)
                            sp.wait_ge(biased, n * BIASED + (4 + NT - V_FIRST))
                            for u in range(2):
                                sp.wait_ge(v_stored[u], n * (8 * NT) + (160 + 16))
                            for v in range(4):
                                if v == 2:
                                    sp.wait_ge(unit_read, n * UNITS + (UNITS + 4))
                                fetch_v(cc, o, 0, v)
                            with sp.Fori(1, NG // 4) as g:
                                for v in range(4):
                                    load_v(cc, o, g, v)
                        elif o == 0 and cc < KC - 1:
                            for g in range(NG // 4):
                                for v in range(4):
                                    load_v(cc, o, g, v)
                                for p in RES[g]:
                                    load_residual(cc + 1, p)
                        else:
                            with sp.Fori(0, NG // 4) as g:
                                for v in range(4):
                                    load_v(cc, o, g, v)
            sp.wait_ge(gram_added, N * KC + 1)
            sp.dma_start(gram_dram[:, :].rearrange("(k p) c -> p k c", p=P), gram_sb[:, :, :]).then_inc(gram_out, 16)
            sp.wait_ge(gram_out, 16)
            for u in range(2):
                for p in range(YP):
                    sp.wait_ge(y_stored[u][p], N * (KC // 2 * 16) + 16)
            g_rows = gram_dram[:, :].rearrange("(k b i) c -> b k i c", k=KC, b=BPC)
            for b in range(BPC):
                sp.dma_start(g_cov[b:GROUPS:BPC, :, :], g_rows[b, :, :, b * GS:(b + 1) * GS]).then_inc(gram_in, 16)
                sp.dma_start(g_sum[b:GROUPS:BPC, :].unsqueeze(2), g_rows[b, :, :, 2 * P:2 * P + 1], allow_slow_non_contiguous=True).then_inc(gram_in, 16)
            sp.wait_ge(fact_made, 1)
            sp.dma_start(wmat_dram[:, :, :], g_wt).then_inc(fact_out, 16)
            sp.dma_start(wbias_dram[:, :], g_bias).then_inc(fact_out, 16)
            sp.wait_ge(fact_out, 32)
            sp.wait_ge(wmat_zero, 1)
            for b in range(BPC):
                sp.dma_start(wmat[b * GS:(b + 1) * GS, :, b * GS:(b + 1) * GS],
                             wmat_dram[:, :, :].rearrange("(k b) j i -> b j k i", b=BPC)[b]).then_inc(fact_in, 16)
            sp.dma_start(wbias, wbias_dram[:, :].rearrange("(k b) i -> (b i) k", b=BPC), allow_slow_non_contiguous=True).then_inc(fact_in, 16)
            with sp.Fori(0, N) as n:
                for cc in range(KC):
                    for f in range(FN):
                        u = f % 2
                        sp.wait_ge(fin_ready[1], (n * (KC * FN) + (cc * FN + f + 1)) * HFB)
                        sp.dma_start(fy[:, u, :], y_dram[n, cc, :, f * FT:(f + 1) * FT]).then_inc(fy_loaded[u], 16)
            for u in range(2):
                sp.wait_ge(out_stored[u], 16 * N * KC * FN // 2 + 16)

        @block.gpsimd
        def _(pool):
            pool.memset(ident[:, :], 1.0).then_inc(consts_made, 1)
            pool.memset(gram_sb[:, :, :], 0.0).then_inc(consts_made, 1)
            pool.memset(ones_sq, 1.0).then_inc(consts_made, 1)
            pool.memset(ones_row[:, :], 1.0).then_inc(consts_made, 1)
            pool.memset(off_diag[:, :], 1.0).then_inc(consts_made, 1)
            pool.wait_ge(consts_made, 5)
            pool.affine_select(out=ident[:, :], in_=ident[:, :], compare_op=ALU.is_equal, fill=0.0, base=0,
                               pattern=[[-1, P]], channel_multiplier=1).then_inc(consts_made, 1)
            pool.affine_select(out=off_diag[:, :], in_=off_diag[:, :], compare_op=ALU.not_equal, fill=0.0, base=0,
                               pattern=[[-1, H]], channel_multiplier=1).then_inc(consts_made, 1)
            pool.wait_ge(consts_made, 7)
            with pool.Fori(0, N) as n:
                def low_part(t, u, q):
                    pool.wait_ge(xs_hi, n * UNITS + t * SUB + (q + 1))
                    pool.tensor_tensor(xs[:, q, 1, :, :], xt[:, u, :, q::SUB], xs[:, q, 0, :, :].bitcast(F32),
                                       ALU.subtract).then_inc(xs_lo, 1)

                def stage(i, v):
                    pool.wait_ge(factors, n * 2 + 2)
                    pool.wait_ge(bank_ready, n * BANK_USES + i * TPT + (v + 1))
                    l = i * (TPT * RT) + v * RT
                    pool.tensor_tensor(pstage[:, v, :, :], att_lines[:, ds(l, RT), :],
                                       factor[:, ds(l, RT)].unsqueeze(2).broadcast_to([H, RT, H]),
                                       ALU.mult).then_inc(staged, 1)

                for t in range(V_FIRST + 1):
                    for q in range(SUB):
                        low_part(t, t % 2, q)
                with pool.Fori(0, NG) as g:
                    pool.wait_ge(exp_done, n * 2 * NG + g + (NG + 1))
                    cols = att4[:, 1, ds(g * R, R), :]
                    pool.tensor_tensor(cols, cols, off_diag[:, :].unsqueeze(1).broadcast_to([H, R, H]), ALU.mult).then_inc(masked, 1)
                with pool.Fori(V_FIRST // 2, D_TURN // 2) as j:
                    for u in (1, 0):
                        for q in range(SUB):
                            low_part(j * 2 + (2 - u), u, q)
                with pool.Fori(0, (NT - D_TURN) // 2 - 1) as j:
                    for u in range(2):
                        for v in range(TPT):
                            stage(j * 2 + u, v)
                        for q in range(SUB):
                            low_part(j * 2 + (D_TURN + u + 1), 1 - u, q)
                for v in range(TPT):
                    stage(NT - 2 - D_TURN, v)
                for q in range(SUB):
                    low_part(NT - 1, 1, q)
                for v in range(TPT):
                    stage(NT - 1 - D_TURN, v)

        @block.scalar
        def _(act):
            act.sem_inc(qk_free, 2)
            act.sem_inc(biased, 4)
            for u in range(2):
                act.sem_inc(v_stored[u], 16)
                for p in range(YP):
                    act.sem_inc(y_stored[u][p], 16)
                act.sem_inc(out_stored[u], 16)
            act.sem_inc(fin_free[0], 2)
            act.wait_ge(weights_scaled, 1)
            nc.scalar.copy(wv_hi[:, :, :], wv_gam).then_inc(weights_hi, 1)
            nc.scalar.activation(wqk_abs, wqk[:, :, :], ACT.Abs)
            nc.scalar.activation(bqk_abs, bias_qk, ACT.Abs)
            nc.scalar.activation(wv_abs, wv_gam, ACT.Abs).then_inc(weights_abs, 1)
            with act.Fori(0, N) as n:
                def high_part(t, u, q, load):
                    act.wait_ge(x_loaded[u], n * (NT * 8) + load * 16)
                    act.wait_ge(unit_read, n * UNITS + t * SUB + (q + 3))
                    nc.scalar.copy(xs[:, q, 0, :, :], xt[:, u, :, q::SUB]).then_inc(xs_hi, 1)

                def split_next(t, u):
                    for q in range(SUB):
                        high_part(t + 1, 1 - u, q, (t + 1) // 2 + 1)

                def values_high(t, u, store):
                    act.wait_ge(unit_read, n * UNITS + t * SUB + (SUB + 4))
                    act.wait_ge(v_stored[u], n * (8 * NT) + store * 16 + 16)
                    nc.scalar.activation(vout[:, u, :, :, 0, :].rearrange("p k s c -> p s k c"),
                                         pair[:, u, :, :].rearrange("p s (k c) -> p s k c", c=P),
                                         ACT.Identity, scale=v_up).then_inc(v_high, 1)

                def store_v(t, u, place=PAIR_V):
                    act.wait_ge(pair_free, n * PAIR_USES + t + (place + 3))
                    act.dma_start(v_tile[n, ds(t * P, P), :, :],
                                  vout[:, u, :, :, :, :].rearrange("p k s h c -> p k (s h c)")).then_inc(v_stored[u], 16)

                def turned_high(i, v):
                    act.wait_ge(bank_ready, n * BANK_USES + i * TPT + (v + 3))
                    nc.scalar.activation(att_parts[:, ds(i * (TPT * RT) + v * RT, RT), 0, :],
                                         bank[0:H, v, 0:RT * H].rearrange("p (r i) -> p r i", i=H),
                                         ACT.Copy, scale=ATT_UP).then_inc(bank_high, 1)

                def residual(t, u):
                    for cc in range(2):
                        last = nc.scalar.activation(qk[:, cc, ds(t * TP, TP)], xt[:, u, cc, :], ACT.Identity,
                                                    bias=out_bias[:, cc:cc + 1])
                    last.then_inc(biased, 1)

                for a, b in ((0, NQ // 2 - 3), (NQ // 2 - 3, NQ // 2)):
                    with act.Fori(a, b) as j:
                        for u in range(2):
                            t = j * 2 + u
                            act.wait_ge(qk_ready, n * NQ + t + 1)
                            nc.scalar.activation(qk_raw[:, ds(t * TQ, TQ)], bank[:, u, 0:TQ], ACT.Identity,
                                                 bias=bias_qk).then_inc(qk_free, 1)
                    if a == 0:
                        for q in range(SUB):
                            high_part(0, 0, q, 1)

                def qk_parts(i):
                    nc.scalar.activation(qk_hi[:, i * PX:(i + 1) * PX], qk_raw[:, i * PX:(i + 1) * PX],
                                         ACT.Identity, scale=qk_up).then_inc(qk_high, 1)

                def move(i, part, moved):
                    act.dma_start(moved[0:D, i * PX:(i + 1) * PX], part[D:2 * D, i * PX:(i + 1) * PX]).then_inc(keys_moved[i], 16)

                def move_high(i):
                    act.wait_ge(qk_high, n * QP + (i + 1))
                    move(i, qk_hi, k_hi)

                def move_low(i):
                    act.wait_ge(qk_low, n * QP + (i + 1))
                    move(i, qk_lo, k_lo)

                for u in range(2):
                    for p in range(YP):
                        act.wait_ge(y_stored[u][p], n * (KC // 2 * 16) + 16)
                act.wait_ge(qk_free, n * NQ + (NQ + 2))
                act.wait_ge(bounds_done, n + 1)
                for t in range(V_FIRST):
                    for i in range(t * QP // V_FIRST, (t + 1) * QP // V_FIRST):
                        qk_parts(i)
                        if i > 0:
                            move_high(i - 1)
                        if i > 1:
                            move_low(i - 2)
                    split_next(t, t % 2)
                    values_high(t, t % 2, 0)
                move_high(QP - 1)
                move_low(QP - 2)
                move_low(QP - 1)
                for t in range(V_FIRST):
                    store_v(t, t % 2, 0)
                with act.Fori(0, 2 * NG) as g:
                    act.wait_ge(pair_free, n * PAIR_USES + g + (V_FIRST + 3))
                    flat = att[0:H, :, :].rearrange("p o i -> p (o i)")[:, ds(g * R * H, R * H)]
                    nc.scalar.activation(flat, flat, ACT.Exp, scale=e_down[0:H, :]).then_inc(exp_done, 1)
                act.dma_start(qk[:, :, 0:V_FIRST * TP], x_px[n, :, 0:2, 0:V_FIRST * TP]).then_inc(edge_loaded, 16)
                residual(V_FIRST, 0)
                split_next(V_FIRST, 0)
                values_high(V_FIRST, 0, 1)
                act.wait_ge(edge_loaded, n * 16 + 16)
                for cc in range(2):
                    nc.scalar.activation(qk[:, cc, 0:V_FIRST * TP], qk[:, cc, 0:V_FIRST * TP], ACT.Identity,
                                         bias=out_bias[:, cc:cc + 1])
                with act.Fori(V_FIRST // 2, D_STAT // 2 - 1) as j:
                    for u in (1, 0):
                        t = j * 2 + (2 - u)
                        residual(t, u)
                        for q in range(SUB):
                            high_part(t + 1, 1 - u, q, j + 2)
                        values_high(t, u, j + (1 - u))
                        store_v(t - 1, 1 - u)
                for t in range(D_STAT - 1, D_TURN):
                    if t == D_STAT:
                        act.wait_ge(shift_done, n * 2 + 2)
                        nc.scalar.activation(shifted, shifted, ACT.Exp, scale=e_down[0:H, :]).then_inc(shift_exp, 1)
                    residual(t, t % 2)
                    split_next(t, t % 2)
                    values_high(t, t % 2, t // 2)
                    store_v(t - 1, 1 - t % 2)
                with act.Fori(0, (NT - D_TURN) // 2 - 1) as j:
                    for u in range(2):
                        t = j * 2 + (D_TURN + u)
                        residual(t, u)
                        for q in range(SUB):
                            high_part(t + 1, 1 - u, q, j + (D_TURN // 2 + 1 + u))
                        values_high(t, u, j + D_TURN // 2)
                        store_v(t - 1, 1 - u)
                        for v in range(TPT):
                            turned_high(j * 2 + u, v)
                for t in range(NT - 2, NT):
                    residual(t, t % 2)
                    if t + 1 < NT:
                        split_next(t, t % 2)
                    values_high(t, t % 2, t // 2)
                    store_v(t - 1, 1 - t % 2)
                    if t + 1 == NT:
                        store_v(t, t % 2)
                    for v in range(TPT):
                        turned_high(t - D_TURN, v)
                for cc in range(KC):
                    cu = cc % 2
                    if 0 < cc < KC - 1:
                        act.wait_ge(acc_loaded[1 - cu], n * (YP * 16) + YP * 16)
                        nc.scalar.activation(qk[:, 1 - cu, :], qk[:, 1 - cu, :], ACT.Identity,
                                             bias=out_bias[:, cc + 1:cc + 2]).then_inc(biased, 1)
                    for p in range(YP):
                        if p == 0:
                            act.wait_ge(pair_free, n * PAIR_USES + (PAIR_A + 2 + (cc + 1) * 2 * NG))
                        act.dma_start(y_dram[n, cc, :, p * Y_PIECE:(p + 1) * Y_PIECE],
                                      qk[:, cu, p * Y_PIECE:(p + 1) * Y_PIECE]).then_inc(y_stored[cu][p], 16)
                        for u in range(3):
                            act.wait_ge(bank_ready, n * BANK_USES + (BANK_G + cc * NB + p * 3 + u + 3))
                            act.wait_ge(ytr_free, n * (KC * NB) + (cc * NB + p * 3 + u + 1))
                            nc.scalar.activation(ytr_slots[u][:, :, 0:P], turn_ps[u].rearrange("p (s c) -> p s c", c=P),
                                                 ACT.Copy, scale=y_up).then_inc(bank_high, 1)
            act.wait_ge(gram_out, 16)
            for u in range(2):
                for p in range(YP):
                    act.wait_ge(y_stored[u][p], N * (KC // 2 * 16) + 16)
            for b in range(BPC):
                act.dma_start(g_low[b:GROUPS:BPC, :, :],
                              gram_dram[:, :].rearrange("(k b i) c -> b k i c", k=KC, b=BPC)[b, :, :, P + b * GS:P + (b + 1) * GS]
                              ).then_inc(gram_in, 16)
            act.wait_ge(sq_ready, 1)
            nc.scalar.activation(g_rt, g_piv, ACT.Sqrt).then_inc(sq_done, 1)
            act.wait_ge(fact_in, 16 * (BPC + 1))
            with act.Fori(0, N) as n:
                for cc in range(KC):
                    for f in range(FN):
                        u = f % 2
                        act.wait_ge(out_stored[u], (n * (KC * FN // 2) + (cc * FN // 2 + f // 2 + 1)) * 16)
                        for b in range(HFB):
                            act.wait_ge(fin_ready[0], n * (KC * FN * HFB) + ((cc * FN + f) * HFB + b + 1))
                            nc.scalar.activation(fo[:, u, 2 * b * FB:(2 * b + 1) * FB], bank[:, (f * HFB + b) % 2, 0:FB],
                                                 ACT.Identity, bias=wbias[:, cc:cc + 1]).then_inc(fin_free[0], 1)
                        for e in range(2):
                            act.wait_ge(fin_free[e], n * (KC * FN * HFB) + ((cc * FN + f + 1) * HFB + 2))
                        act.dma_start(out_px[n, cc, :, f * FT:(f + 1) * FT],
                                      fo[:, u, :]).then_inc(out_stored[u], 16)

        @block.vector
        def _(dve):
            nc.vector.sem_inc(pair_free, 2)
            nc.vector.sem_inc(bank_free, 2)
            nc.vector.sem_inc(gram_added, 1)
            nc.vector.sem_inc(fin_free[1], 2)
            steps = [0]

            def link(ins):
                steps[0] += 1
                ins.then_inc(chain, 1)
                dve.wait_ge(chain, steps[0])

            dve.wait_ge(consts_loaded, 8 * 16)
            nc.vector.tensor_scalar(wv_gam, wv_raw, gam, None, ALU.mult).then_inc(weights_scaled, 1)
            nc.vector.memset(ytr[:, :, :, 2 * P:GC], 1.0)
            nc.vector.tensor_scalar(out_bias, out_bias, gam, None, ALU.mult)
            link(nc.vector.tensor_scalar(bv_rep, bv_rep, gam, None, ALU.mult))
            link(nc.vector.tensor_reduce(bv_top, bv_rep, AX.X, ALU.max, apply_absolute_value=True))
            dve.wait_ge(weights_hi, 1)
            nc.vector.tensor_tensor(wv_lo[:, :, :], wv_gam, wv_hi[:, :, :].bitcast(F32), ALU.subtract).then_inc(weights_lo, 1)
            dve.wait_ge(norm_ready, 1)
            link(nc.vector.tensor_reduce(w_norm, stat_ps[:, 0:C], AX.X, ALU.max))
            link(nc.vector.tensor_reduce(wqk_norm, gram_ps[:, 0:2 * D], AX.X, ALU.max))
            link(nc.vector.tensor_scalar(bqk_sum, gram_ps[:, 2 * D:2 * D + 1], 1e-20, None, ALU.max))
            dve.wait_ge(consts_made, 7)
            with dve.Fori(0, N) as n:
                def values_low(t, u):
                    dve.wait_ge(v_high, n * NT + t + 1)
                    for q in range(SUB):
                        last = nc.vector.scalar_tensor_tensor(
                            vout[:, u, :, q, 1, :], pair[:, u, q, :].rearrange("p (k c) -> p k c", c=P), v_up,
                            vout[:, u, :, q, 0, :], ALU.mult, ALU.subtract)
                    last.then_inc(pair_free, 1)

                def turned_low(i, v):
                    dve.wait_ge(bank_high, n * BANK_USES + i * TPT + (v + 1))
                    l = i * (TPT * RT) + v * RT
                    nc.vector.scalar_tensor_tensor(
                        att_parts[:, ds(l, RT), 1, :], bank[0:H, v, 0:RT * H].rearrange("p (r i) -> p r i", i=H), ATT_UP,
                        att_parts[:, ds(l, RT), 0, :], ALU.mult, ALU.subtract).then_inc(bank_free, 1)

                def small(k, ins, base):
                    ins.then_inc(chain, 1)
                    dve.wait_ge(chain, n * (SMALL + BOUNDS) + (CHAIN0 + base + k))

                with dve.Fori(0, NQ // QS) as j:
                    for u in range(QS):
                        dve.wait_ge(xq_loaded[u], n * (NQ // QS * 16) + j * 16 + 16)
                        nc.vector.tensor_reduce(xmax[:, ds(j * QS + u, 1)], xq[:, u, :, :], AX.XY, ALU.max,
                                                apply_absolute_value=True).then_inc(x_seen, 1)
                dve.wait_ge(x_seen, n * NQ + NQ)
                nc.vector.tensor_reduce(x_col, xmax[:, :], AX.X, ALU.max).then_inc(bound_m, 1)
                dve.wait_ge(bound_t, n * 2 + 1)
                nc.vector.tensor_reduce(x_top[0:1, :], stat_ps[0:1, 0:P], AX.X, ALU.max).then_inc(bound_m, 1)
                dve.wait_ge(bound_t, n * 2 + 2)
                small(1, nc.vector.tensor_copy(x_top, stat_ps[:, P:P + 1]), 0)
                small(2, nc.vector.tensor_scalar(v_top, x_top, w_norm, 1e-20, ALU.mult, ALU.max), 0)
                small(3, nc.vector.tensor_scalar(qk_top, x_top, wqk_norm, bqk_sum, ALU.mult, ALU.add), 0)
                small(4, nc.vector.reciprocal(qk_up, qk_top), 0)
                small(5, nc.vector.tensor_scalar(qk_up, qk_up, HALF_TOP, None, ALU.mult), 0)
                small(6, nc.vector.tensor_scalar(e_down, qk_top, 1.0 / HALF_TOP, None, ALU.mult), 0)
                small(7, nc.vector.tensor_tensor(e_down, e_down, e_down, ALU.mult), 0)
                small(8, nc.vector.tensor_scalar(y_top, x_top, v_top, bv_top, ALU.add, ALU.add), 0)
                small(9, nc.vector.reciprocal(v_up, v_top), 0)
                small(10, nc.vector.reciprocal(y_up, y_top), 0)
                small(11, nc.vector.tensor_scalar(v_up, v_up, HALF_TOP, None, ALU.mult), 0)
                small(12, nc.vector.tensor_scalar(y_up, y_up, HALF_TOP, None, ALU.mult), 0)
                small(13, nc.vector.tensor_scalar(y_down, y_top, 1.0 / HALF_TOP, None, ALU.mult), 0)
                small(14, nc.vector.tensor_scalar(v_down, v_top, 1.0 / (HALF_TOP * ATT_UP), None, ALU.mult), 0)
                nc.vector.tensor_tensor(y_down2, y_down, y_down, ALU.mult).then_inc(bounds_done, 1)
                dve.wait_ge(qk_free, n * NQ + (NQ + 2))
                for t in range(V_FIRST):
                    for i in range(t * QP // V_FIRST, (t + 1) * QP // V_FIRST):
                        dve.wait_ge(qk_high, n * QP + (i + 1))
                        nc.vector.scalar_tensor_tensor(qk_lo[:, i * PX:(i + 1) * PX], qk_raw[:, i * PX:(i + 1) * PX], qk_up,
                                                       qk_hi[:, i * PX:(i + 1) * PX], ALU.mult, ALU.subtract).then_inc(qk_low, 1)
                    values_low(t, t % 2)
                for o in range(2):
                    mx = max_r if o == 0 else max_c
                    with dve.Fori(0, NG // GE) as g:
                        for u in range(GE + 1):
                            if u < GE:
                                dve.wait_ge(pair_ready, n * PAIR_READY + g * GE + (o * NG + u + 1))
                                nc.vector.tensor_reduce(mx[:, ds((g * GE + u) * R, R)], pair_lines((u + 2) % 3)[0:H], AX.X,
                                                        ALU.max).then_inc(group_max, 1)
                            if u > 0:
                                l = (g * GE + (u - 1)) * R
                                dve.wait_ge(group_max, n * 2 * NG + g * GE + (o * NG + u))
                                nc.vector.tensor_tensor(att4[:, o, ds(l, R), :], pair_lines((u + 1) % 3)[0:H],
                                                        mx[:, ds(l, R)].unsqueeze(2).broadcast_to([H, R, H]),
                                                        ALU.subtract).then_inc(pair_free, 1)
                for t in range(V_FIRST, D_STAT):
                    for e in range(SUMS):
                        o, g = divmod((t - V_FIRST) * SUMS + e, NG)
                        if o == 0:
                            dve.wait_ge(exp_done, n * 2 * NG + (g + 1))
                        else:
                            dve.wait_ge(masked, n * NG + (g + 1))
                        nc.vector.tensor_reduce((sum_r, sum_c)[o][:, g * R:(g + 1) * R], att4[:, o, g * R:(g + 1) * R, :],
                                                AX.X, ALU.add).then_inc(sums_done, 1)
                    values_low(t, t % 2)

                dve.wait_ge(stat_t, n * 2 + 1)
                max_ct, sum_ct, fac_ps = (stat_ps[0:H, i * H:(i + 1) * H] for i in range(3))
                small(1, nc.vector.tensor_tensor(joint, max_r, max_ct, ALU.max), BOUNDS)
                nc.vector.tensor_tensor(shifted[:, 0, :], max_r, joint, ALU.subtract).then_inc(shift_done, 1)
                nc.vector.tensor_tensor(shifted[:, 1, :], max_ct, joint, ALU.subtract).then_inc(shift_done, 1)
                dve.wait_ge(shift_exp, n + 1)
                nc.vector.tensor_tensor(fac_r, sum_r, shifted[:, 0, :], ALU.mult).then_inc(chain, 1)
                small(3, nc.vector.tensor_tensor(fac_ct, sum_ct, shifted[:, 1, :], ALU.mult), BOUNDS)
                small(4, nc.vector.tensor_tensor(joint, fac_r, fac_ct, ALU.add), BOUNDS)
                small(5, nc.vector.reciprocal(joint, joint), BOUNDS)
                nc.vector.tensor_tensor(fac_ct, shifted[:, 1, :], joint, ALU.mult).then_inc(chain, 1)
                nc.vector.tensor_tensor(fac_r, shifted[:, 0, :], joint, ALU.mult).then_inc(factors, 1)
                for t in range(D_STAT, D_FAC):
                    values_low(t, t % 2)
                dve.wait_ge(stat_t, n * 2 + 2)
                nc.vector.tensor_copy(fac_c, fac_ps).then_inc(factors, 1)
                for t in range(D_FAC, D_TURN):
                    values_low(t, t % 2)
                with dve.Fori(0, (NT - D_TURN) // 2) as j:
                    for u in range(2):
                        values_low(j * 2 + (D_TURN + u), u)
                        for v in range(TPT):
                            turned_low(j * 2 + u, v)
                nc.vector.memset(ytr_slots[2][:, :, 2 * P:GC], 1.0)
                for cc in range(KC):
                    cu = cc % 2
                    ready = 4 + NT - V_FIRST + max(cc - 1, 0)
                    for o in range(2):
                        with dve.Fori(0, NG // 3) as g:
                            if o == 0:
                                dve.wait_ge(biased, n * BIASED + ready)
                            else:
                                dve.wait_ge(pair_free, n * PAIR_USES + (PAIR_A + 2 + (2 * cc + 1) * NG))
                            for u in range(3):
                                dve.wait_ge(pair_ready, n * PAIR_READY + g * 3 + (READY_A + (2 * cc + o) * NG + u + 1))
                                l = (g * 3 + u) * R
                                dst = acc4[:, cu, ds(l, R), :] if o == 0 else acc4[:, cu, :, ds(l, R)].rearrange("p y r -> p r y")
                                nc.vector.scalar_tensor_tensor(dst, pair_lines(u), v_down, dst, ALU.mult, ALU.add).then_inc(pair_free, 1)
                    with dve.Fori(0, NB // 3) as j:
                        for u in range(3):
                            dve.wait_ge(bank_high, n * BANK_USES + j * 3 + (BANK_G + cc * NB + u + 1))
                            nc.vector.scalar_tensor_tensor(ytr_slots[u][:, :, P:2 * P], turn_ps[u].rearrange("p (s c) -> p s c", c=P),
                                                           y_up, ytr_slots[u][:, :, 0:P], ALU.mult, ALU.subtract).then_inc(bank_free, 1)
                    dve.wait_ge(ytr_free, n * (KC * NB) + ((cc + 1) * NB + 3))
                    nc.vector.scalar_tensor_tensor(gram_sb[:, cc, 2 * P:GC], gram_ps[:, 2 * P:GC], y_down,
                                                   gram_sb[:, cc, 2 * P:GC], ALU.mult, ALU.add)
                    nc.vector.scalar_tensor_tensor(gram_sb[:, cc, 0:2 * P], gram_ps[:, 0:2 * P], y_down2,
                                                   gram_sb[:, cc, 0:2 * P], ALU.mult, ALU.add).then_inc(gram_added, 1)
            steps[0] = CHAIN0 + N * (SMALL + BOUNDS)
            INV = 1.0 / (N * HW)
            dve.wait_ge(gram_in, 48 * BPC)
            link(nc.vector.tensor_tensor(g_cov, g_cov, g_low, ALU.add))
            link(nc.vector.tensor_tensor(g_cov, g_cov, g_low.rearrange("p i j -> p j i"), ALU.add))
            link(nc.vector.tensor_scalar(g_mean, g_sum, INV, None, ALU.mult))
            link(nc.vector.tensor_tensor(g_tmp, g_mean.unsqueeze(2).broadcast_to([GROUPS, GS, GS]),
                                         g_mean.unsqueeze(1).broadcast_to([GROUPS, GS, GS]), ALU.mult))
            link(nc.vector.tensor_scalar(g_cov, g_cov, INV, None, ALU.mult))
            link(nc.vector.tensor_tensor(g_cov, g_cov, g_tmp, ALU.subtract))
            link(nc.vector.memset(g_eye, 0.0))
            link(nc.vector.memset(qk[0:GROUPS, 0, 3072:3072 + GS * GS:GS + 1], 1.0))
            link(nc.vector.tensor_scalar(g_aug[:, :, 0:GS], g_cov, 1.0 - EPS, None, ALU.mult))
            link(nc.vector.tensor_scalar(g_tmp, g_eye, EPS, None, ALU.mult))
            link(nc.vector.tensor_tensor(g_aug[:, :, 0:GS], g_aug[:, :, 0:GS], g_tmp, ALU.add))
            link(nc.vector.tensor_copy(g_aug[:, :, GS:2 * GS], g_eye))
            for k in range(GS - 1):
                m = GS - 1 - k
                link(nc.vector.reciprocal(g_rec, g_aug[:, k, k:k + 1]))
                link(nc.vector.tensor_scalar(g_fac[:, 0:m].unsqueeze(2), g_aug[:, k + 1:GS, k:k + 1], g_rec, None, ALU.mult))
                link(nc.vector.tensor_tensor(g_tmp[:, 0:m, :], g_fac[:, 0:m].unsqueeze(2).broadcast_to([GROUPS, m, GS]),
                                             g_aug[:, k, k + 1:k + 1 + GS].unsqueeze(1).broadcast_to([GROUPS, m, GS]), ALU.mult))
                link(nc.vector.tensor_tensor(g_aug[:, k + 1:GS, k + 1:k + 1 + GS], g_aug[:, k + 1:GS, k + 1:k + 1 + GS],
                                             g_tmp[:, 0:m, :], ALU.subtract))
            nc.vector.tensor_copy(g_piv, qk[0:GROUPS, 0, 1024:1024 + 2 * GS * GS:2 * GS + 1]).then_inc(sq_ready, 1)
            dve.wait_ge(sq_done, 1)
            link(nc.vector.reciprocal(g_piv, g_rt))
            link(nc.vector.tensor_tensor(g_wt, g_aug[:, :, GS:2 * GS].rearrange("p i j -> p j i"),
                                         g_piv.unsqueeze(1).broadcast_to([GROUPS, GS, GS]), ALU.mult))
            link(nc.vector.tensor_tensor(g_tmp, g_wt.rearrange("p j i -> p i j"),
                                         g_mean.unsqueeze(1).broadcast_to([GROUPS, GS, GS]), ALU.mult))
            nc.vector.tensor_reduce(g_bias, g_tmp, AX.X, ALU.add, negate=True).then_inc(fact_made, 1)
            nc.vector.memset(wmat, 0.0).then_inc(wmat_zero, 1)
            dve.wait_ge(fact_in, 16 * (BPC + 1))
            with dve.Fori(0, N) as n:
                for cc in range(KC):
                    for f in range(FN):
                        u = f % 2
                        dve.wait_ge(out_stored[u], (n * (KC * FN // 2) + (cc * FN // 2 + f // 2 + 1)) * 16)
                        for b in range(HFB):
                            dve.wait_ge(fin_ready[1], n * (KC * FN * HFB) + ((cc * FN + f + 2) * HFB + b + 1))
                            nc.vector.tensor_scalar(fo[:, u, (2 * b + 1) * FB:(2 * b + 2) * FB],
                                                    pair[:, (f * HFB + b) % 2, 0, 0:FB],
                                                    wbias[:, cc:cc + 1], None, ALU.add).then_inc(fin_free[1], 1)

        @block.tensor
        def _(pe):
            pe.sem_inc(unit_read, 4)
            pe.sem_inc(ytr_free, 3)
            pe.wait_ge(consts_loaded, 8 * 16)
            pe.sem_inc(bank_ready, 2)
            pe.wait_ge(weights_lo, 1)
            pe.wait_ge(consts_made, 7)

            pe.wait_ge(weights_abs, 1)
            for k in range(KC):
                last = nc.tensor.matmul(stat_ps[:, 0:C], ones_sq, wv_abs[:, k, :], start=k == 0, stop=k == KC - 1)
            for k in range(KC):
                nc.tensor.matmul(gram_ps[:, 0:2 * D], ones_sq, wqk_abs[:, k, :], start=k == 0, stop=k == KC - 1)
            last = nc.tensor.matmul(gram_ps[:, 2 * D:2 * D + 1], ones_sq, bqk_abs, start=True, stop=True)
            last.then_inc(norm_ready, 1)

            with pe.Fori(0, N) as n:
                def project_v(t, u, place=PAIR_V):
                    pe.wait_ge(pair_free, n * PAIR_USES + t + (place + 1))
                    for q in range(SUB):
                        pe.wait_ge(xs_lo, n * UNITS + t * SUB + (q + 1))
                        terms = [(xs[:, q, a, k, :], w[:, k, :]) for k in range(KC)
                                 for a, w in ((1, wv_hi), (0, wv_lo), (0, wv_hi))]
                        for i, (lhs, rhs) in enumerate(terms):
                            last = nc.tensor.matmul(pair[:, u, q, :], lhs, rhs, start=i == 0, stop=i == len(terms) - 1)
                        last.then_inc(unit_read, 1)

                def project_qk(t, u, load):
                    pe.wait_ge(xq_loaded[u], n * (NQ // QS * 16) + load * 16)
                    pe.wait_ge(bank_free, n * BANK_USES + 2)
                    pe.wait_ge(qk_free, n * NQ + t + 1)
                    for k in range(KC):
                        last = nc.tensor.matmul(bank[:, u % 2, 0:TQ], wqk[:, k, :], xq[:, u, k, :], start=k == 0, stop=k == KC - 1)
                    last.then_inc(qk_ready, 1)

                with pe.Fori(0, NQ // QS - 1) as j:
                    for u in range(QS):
                        project_qk(j * QS + u, u, j + 1)
                for t in range(NQ - QS, NQ):
                    if t == NQ - 2:
                        pe.wait_ge(bound_m, n * 2 + 1)
                        nc.tensor.transpose(stat_ps[0:1, 0:P], x_col, ident[:, :]).then_inc(bound_t, 1)
                    if t == NQ - 1:
                        pe.wait_ge(bound_m, n * 2 + 2)
                        nc.tensor.matmul(stat_ps[:, P:P + 1], ones_row[:, :], x_top[0:1, :], start=True, stop=True).then_inc(bound_t, 1)
                    project_qk(t, t % QS, NQ // QS)
                pe.wait_ge(qk_free, n * NQ + (NQ + 2))
                for t in range(V_FIRST):
                    project_v(t, t % 2, 0)
                for e in range(2 * NG):
                    o, g = divmod(e, NG)
                    if e < NG and e % (NG // QP) == 0:
                        pe.wait_ge(qk_low, n * QP + (e // (NG // QP) + 1))
                        pe.wait_ge(keys_moved[e // (NG // QP)], n * 32 + 32)
                    pe.wait_ge(pair_free, n * PAIR_USES + (V_FIRST + e))
                    for r in range(R):
                        l = g * R + r
                        parts = ((qk_lo, k_hi), (qk_hi, k_lo), (qk_hi, k_hi))
                        for i, (q, k) in enumerate(parts):
                            last = nc.tensor.matmul(pair_lines((e + 2) % 3)[0:H, r, :], qk_line(q, o, l), qk_line(k, o, l), start=i == 0, stop=i == 2)
                    last.then_inc(pair_ready, 1)

                with pe.Fori(V_FIRST // 2, D_STAT // 2) as j:
                    for u in range(2):
                        project_v(j * 2 + u, u)
                pe.wait_ge(sums_done, n * 2 * NG + 2 * NG)
                nc.tensor.transpose(stat_ps[0:H, 0:H], max_c, ident[0:H, 0:H])
                nc.tensor.transpose(stat_ps[0:H, H:2 * H], sum_c, ident[0:H, 0:H]).then_inc(stat_t, 1)
                for t in range(D_STAT, D_FAC):
                    project_v(t, t % 2)
                pe.wait_ge(chain, n * (SMALL + BOUNDS) + (CHAIN0 + BOUNDS + 6))
                nc.tensor.transpose(stat_ps[0:H, 2 * H:3 * H], fac_ct, ident[0:H, 0:H]).then_inc(stat_t, 1)
                for t in range(D_FAC, D_TURN):
                    project_v(t, t % 2)
                with pe.Fori(0, (NT - D_TURN) // 2) as j:
                    for u in range(2):
                        project_v(j * 2 + (D_TURN + u), u)
                        for v in range(TPT):
                            pe.wait_ge(staged, n * NTR + j * (2 * TPT) + (u * TPT + v + 1))
                            pe.wait_ge(bank_free, n * BANK_USES + j * (2 * TPT) + (u * TPT + v + 1))
                            for r in range(RT):
                                last = nc.tensor.transpose(bank[0:H, v, r * H:(r + 1) * H], pstage[:, v, r, :], ident[0:H, 0:H])
                            last.then_inc(bank_ready, 1)

                with pe.Fori(0, KC // 2) as cp:
                    for cu in range(2):
                        for a in range(2 * NG):
                            o, g = divmod(a, NG)
                            v = g % 4
                            if a == 0:
                                pe.wait_ge(bank_free, n * BANK_USES + (BANK_G + 2))
                            pe.wait_ge(v_loaded[v], n * (KC * NG // 2 * 16) + cp * (NG * 16) + (cu * (NG // 2) + a // 4 + 1) * 16)
                            if a < 3:
                                pe.wait_ge(pair_free, n * PAIR_USES + cp * (4 * NG) + (PAIR_A + cu * 2 * NG + 2))
                                pe.wait_ge(bank_free, n * BANK_USES + cp * (2 * NB) + (BANK_G + cu * NB + 2))
                            else:
                                pe.wait_ge(pair_free, n * PAIR_USES + cp * (4 * NG) + (PAIR_A + cu * 2 * NG + a))
                            for r in range(R):
                                for i, (vh, ah) in enumerate(((1, 0), (0, 1), (0, 0))):
                                    last = nc.tensor.matmul(pair_lines(a % 3)[:, r, :],
                                                            vin[v][0:H, r, vh * P:(vh + 1) * P],
                                                            att_parts[:, a * R + r, ah, :], start=i == 0, stop=i == 2)
                            last.then_inc(pair_ready, 1)

                        def turn(b):
                            if b == 0:
                                pe.wait_ge(pair_free, n * PAIR_USES + cp * (4 * NG) + (PAIR_A + 2 + (cu + 1) * 2 * NG))
                            pe.wait_ge(bank_free, n * BANK_USES + cp * (2 * NB) + (BANK_G + cu * NB + max(b, 2)))
                            for s in range(SB):
                                last = nc.tensor.transpose(turn_ps[b % 3][:, s * P:(s + 1) * P],
                                                           qk[:, cu, (b * SB + s) * P:(b * SB + s + 1) * P], ident[:, :])
                            last.then_inc(bank_ready, 1)

                        def products(b):
                            if b == 0:
                                pe.wait_ge(gram_added, n * KC + cp * 2 + (cu + 1))
                            pe.wait_ge(bank_free, n * BANK_USES + cp * (2 * NB) + (BANK_G + cu * NB + b + 3))
                            for s in range(SB):
                                nc.tensor.matmul(gram_ps[:, 0:GC], ytr_slots[b % 3][:, s, 0:P], ytr_slots[b % 3][:, s, :],
                                                 start=b == 0 and s == 0, stop=False, skip_group_check=True)
                                last = nc.tensor.matmul(gram_ps[:, 2 * P:GC], ytr_slots[b % 3][:, s, P:2 * P], ytr_slots[b % 3][:, s, 2 * P:GC],
                                                        start=False, stop=b == NB - 1 and s == SB - 1, skip_group_check=True)
                            last.then_inc(ytr_free, 1)

                        turn(0)
                        turn(1)
                        for b in range(NB):
                            if b + 2 < NB:
                                turn(b + 2)
                            products(b)
            pe.sem_inc(fin_ready[1], 2 * HFB)
            pe.wait_ge(fact_in, 16 * (BPC + 1))
            with pe.Fori(0, N) as n:
                for cc in range(KC):
                    for f in range(FN):
                        u = f % 2
                        pe.wait_ge(fy_loaded[u], (n * (KC * FN // 2) + (cc * FN // 2 + f // 2 + 1)) * 16)
                        for b in range(HFB):
                            for e, dst in enumerate((bank[:, (f * HFB + b) % 2, 0:FB], pair[:, (f * HFB + b) % 2, 0, 0:FB])):
                                pe.wait_ge(fin_free[e], n * (KC * FN * HFB) + ((cc * FN + f) * HFB + b + 1))
                                nc.tensor.matmul(dst, wmat[:, cc, :], fy[:, u, (2 * b + e) * FB:(2 * b + e + 1) * FB],
                                                 start=True, stop=True).then_inc(fin_ready[e], 1)


def kernel(**inputs):
    import concourse.bacc as bacc
    from concourse.bass_utils import run_bass_kernel_spmd

    nc = bacc.Bacc("TRN2", target_bir_lowering=False, num_devices=1)
    arrays = {
        "x": np.ascontiguousarray(inputs["x"]),
        "wq_t": np.ascontiguousarray(np.asarray(inputs["L0_conv_wq"]).T),
        "bq": np.ascontiguousarray(inputs["L0_conv_bq"]),
        "wk_t": np.ascontiguousarray(np.asarray(inputs["L0_conv_wk"]).T),
        "bk": np.ascontiguousarray(inputs["L0_conv_bk"]),
        "wv_t": np.ascontiguousarray(np.asarray(inputs["L0_conv_wv"]).T),
        "bv": np.ascontiguousarray(inputs["L0_conv_bv"]),
        "gamma": np.asarray(inputs["L0_conv_gamma"]).reshape(1),
    }
    args = [nc.dram_tensor(name, a.shape, mybir.dt.from_np(a.dtype), kind="ExternalInput").ap()
            for name, a in arrays.items()]
    out = nc.dram_tensor("out", arrays["x"].shape, mybir.dt.float32, kind="ExternalOutput")
    criss_cross_whitening_kernel(nc, *args, out.ap())
    result = run_bass_kernel_spmd(nc, [arrays], core_ids=[0])
    return result.results[0]["out"]
```
